# Optimizing a Trainium2 kernel written in Bass

```python
import numpy as np
import jax
import jax.numpy as jnp

def _softmax(x, axis=-1):
    return jax.nn.softmax(x, axis=axis)

def _gelu(x):
    return jax.nn.gelu(x, approximate=True)

def _silu(x):
    return jax.nn.silu(x)

def _sigmoid(x):
    return jax.nn.sigmoid(x)

def _layernorm(x, axis=-1, eps=1e-05):
    m = jnp.mean(x, axis=axis, keepdims=True)
    v = jnp.var(x, axis=axis, keepdims=True)
    return (x - m) / jnp.sqrt(v + eps)

def _scatter_add(tgt, idx, src, axis=0):
    return tgt.at[idx].add(src)

def _segment_sum(src, seg, n):
    return jax.ops.segment_sum(src, seg, n)
kernel_name = 'mk_gnn_resnorm_d2_gnn_r32_80eb53'

def setup_inputs(seed: int=0):
    np.random.seed(seed)
    _w = jnp.asarray

    def _rec_inputs():
        import jax
        import jax.numpy as jnp
        _gk = jax.random.key(seed)
        x = -0.000202 + 1 * jax.random.normal(jax.random.fold_in(_gk, 1), (50000, 128), jnp.float32)
        src = jax.random.randint(jax.random.fold_in(_gk, 2), (25000,), 0, 50000, jnp.int32)
        dst = jax.random.randint(jax.random.fold_in(_gk, 3), (25000,), 0, 50000, jnp.int32)
        _o = jnp.argsort(dst, stable=True)
        src = src[_o]
        dst = dst[_o]
        edge_attr_128 = -4.21973e-05 + 0.999841 * jax.random.normal(jax.random.fold_in(_gk, 12), (25000, 128), jnp.float32)
        return (x, src, dst, edge_attr_128)
    x, src, dst, edge_attr_128 = _rec_inputs()

    def _L0_gnn_setup():
        import jax, jax.numpy as jnp
        import numpy as np
        N = 50000
        E = 25000
        IN_DIM = 128
        HID = 128

        def _gin_conv(x, src, dst, W1, b1, W2, b2):
            agg = jax.ops.segment_sum(x[src], dst, num_segments=N)
            h = x + agg
            h = jax.nn.relu(h @ W1 + b1)
            return h @ W2 + b2
        key = jax.random.key(seed)
        ks = jax.random.split(key, 10)
        x = jax.random.normal(ks[0], (N, IN_DIM), dtype=jnp.float32)
        edge_index = jax.random.randint(ks[1], (2, E), 0, N, dtype=jnp.int64)
        s = 1.0 / np.sqrt(IN_DIM)
        s2 = 1.0 / np.sqrt(HID)
        W1a = jax.random.uniform(ks[2], (IN_DIM, HID), jnp.float32, -s, s)
        b1a = jax.random.uniform(ks[3], (HID,), jnp.float32, -s, s)
        W2a = jax.random.uniform(ks[4], (HID, HID), jnp.float32, -s2, s2)
        b2a = jax.random.uniform(ks[5], (HID,), jnp.float32, -s2, s2)
        W1b = jax.random.uniform(ks[6], (HID, HID), jnp.float32, -s2, s2)
        b1b = jax.random.uniform(ks[7], (HID,), jnp.float32, -s2, s2)
        W2b = jax.random.uniform(ks[8], (HID, HID), jnp.float32, -s2, s2)
        b2b = jax.random.uniform(ks[9], (HID,), jnp.float32, -s2, s2)
        return {'x': x, 'edge_index': edge_index, 'W1a': W1a, 'b1a': b1a, 'W2a': W2a, 'b2a': b2a, 'W1b': W1b, 'b1b': b1b, 'W2b': W2b, 'b2b': b2b}
    _L0_gnn_all = _L0_gnn_setup()
    _L0_gnn_in = {k: v for k, v in _L0_gnn_all.items() if k in ('W1a', 'b1a', 'W2a', 'b2a', 'W1b', 'b1b', 'W2b', 'b2b')}
    del _L0_gnn_all

    def _L1_gnn_setup():
        import jax, jax.numpy as jnp
        import numpy as np
        N_NODES = 50000
        N_EDGES = 18750
        DIM = 128
        LN_EPS = 1e-05

        def _linear_params(key, fan_in, fan_out):
            kw, kb = jax.random.split(key)
            bound = 1.0 / np.sqrt(fan_in)
            W = jax.random.uniform(kw, (fan_in, fan_out), minval=-bound, maxval=bound, dtype=jnp.float32)
            b = jax.random.uniform(kb, (fan_out,), minval=-bound, maxval=bound, dtype=jnp.float32)
            return (W, b)
        key = jax.random.key(seed)
        ks = jax.random.split(key, 10)
        e = jax.random.normal(ks[0], (N_NODES, DIM), dtype=jnp.float32)
        a = jax.random.normal(ks[1], (N_EDGES, DIM), dtype=jnp.float32)
        src = jax.random.randint(ks[2], (N_EDGES,), 0, N_NODES, dtype=jnp.int32)
        dst = jax.random.randint(ks[3], (N_EDGES,), 0, N_NODES, dtype=jnp.int32)
        Ws, bs = _linear_params(ks[4], DIM, DIM)
        Wd, bd = _linear_params(ks[5], DIM, DIM)
        Wa, ba = _linear_params(ks[6], DIM, DIM)
        Wm, bm = _linear_params(ks[7], DIM, DIM)
        W1, b1 = _linear_params(ks[8], 2 * DIM, DIM)
        W2, b2 = _linear_params(ks[9], DIM, DIM)
        gamma = jnp.ones((DIM,), dtype=jnp.float32)
        beta = jnp.zeros((DIM,), dtype=jnp.float32)
        return dict(e=e, a=a, src=src, dst=dst, Ws=Ws, bs=bs, Wd=Wd, bd=bd, Wa=Wa, ba=ba, Wm=Wm, bm=bm, W1=W1, b1=b1, W2=W2, b2=b2, gamma=gamma, beta=beta)
    _L1_gnn_all = _L1_gnn_setup()
    _L1_gnn_in = {k: v for k, v in _L1_gnn_all.items() if k in ('Ws', 'bs', 'Wd', 'bd', 'Wa', 'ba', 'Wm', 'bm', 'W1', 'b1', 'W2', 'b2', 'gamma', 'beta')}
    del _L1_gnn_all
    return {'x': x, 'src': src, 'dst': dst, 'edge_attr_128': edge_attr_128, 'L0_gnn_W1a': _L0_gnn_in['W1a'], 'L0_gnn_b1a': _L0_gnn_in['b1a'], 'L0_gnn_W2a': _L0_gnn_in['W2a'], 'L0_gnn_b2a': _L0_gnn_in['b2a'], 'L0_gnn_W1b': _L0_gnn_in['W1b'], 'L0_gnn_b1b': _L0_gnn_in['b1b'], 'L0_gnn_W2b': _L0_gnn_in['W2b'], 'L0_gnn_b2b': _L0_gnn_in['b2b'], 'L1_gnn_Ws': _L1_gnn_in['Ws'], 'L1_gnn_bs': _L1_gnn_in['bs'], 'L1_gnn_Wd': _L1_gnn_in['Wd'], 'L1_gnn_bd': _L1_gnn_in['bd'], 'L1_gnn_Wa': _L1_gnn_in['Wa'], 'L1_gnn_ba': _L1_gnn_in['ba'], 'L1_gnn_Wm': _L1_gnn_in['Wm'], 'L1_gnn_bm': _L1_gnn_in['bm'], 'L1_gnn_W1': _L1_gnn_in['W1'], 'L1_gnn_b1': _L1_gnn_in['b1'], 'L1_gnn_W2': _L1_gnn_in['W2'], 'L1_gnn_b2': _L1_gnn_in['b2'], 'L1_gnn_gamma': _L1_gnn_in['gamma'], 'L1_gnn_beta': _L1_gnn_in['beta']}

def reference(x, src, dst, edge_attr_128, L0_gnn_W1a, L0_gnn_b1a, L0_gnn_W2a, L0_gnn_b2a, L0_gnn_W1b, L0_gnn_b1b, L0_gnn_W2b, L0_gnn_b2b, L1_gnn_Ws, L1_gnn_bs, L1_gnn_Wd, L1_gnn_bd, L1_gnn_Wa, L1_gnn_ba, L1_gnn_Wm, L1_gnn_bm, L1_gnn_W1, L1_gnn_b1, L1_gnn_W2, L1_gnn_b2, L1_gnn_gamma, L1_gnn_beta):
    import jax
    import jax.numpy as jnp

    def _L0_gnn_ref(x, edge_index, W1a, b1a, W2a, b2a, W1b, b1b, W2b, b2b):
        import jax, jax.numpy as jnp
        import numpy as np
        N = 50000
        E = 25000
        IN_DIM = 128
        HID = 128

        def _gin_conv(x, src, dst, W1, b1, W2, b2):
            agg = jax.ops.segment_sum(x[src], dst, num_segments=N)
            h = x + agg
            h = jax.nn.relu(h @ W1 + b1)
            return h @ W2 + b2
        src, dst = (edge_index[0], edge_index[1])
        h = jax.nn.relu(_gin_conv(x, src, dst, W1a, b1a, W2a, b2a))
        h = jax.nn.relu(_gin_conv(h, src, dst, W1b, b1b, W2b, b2b))
        return h

    def _L1_gnn_ref(e, a, src, dst, Ws, bs, Wd, bd, Wa, ba, Wm, bm, W1, b1, W2, b2, gamma, beta):
        import jax, jax.numpy as jnp
        import numpy as np
        N_NODES = 50000
        N_EDGES = 18750
        DIM = 128
        LN_EPS = 1e-05

        def _linear_params(key, fan_in, fan_out):
            kw, kb = jax.random.split(key)
            bound = 1.0 / np.sqrt(fan_in)
            W = jax.random.uniform(kw, (fan_in, fan_out), minval=-bound, maxval=bound, dtype=jnp.float32)
            b = jax.random.uniform(kb, (fan_out,), minval=-bound, maxval=bound, dtype=jnp.float32)
            return (W, b)
        gate_logits = e[src] @ Ws + bs + (e[dst] @ Wd + bd) + (a @ Wa + ba)
        msg = jax.nn.sigmoid(gate_logits) * (e[src] @ Wm + bm)
        agg = jax.ops.segment_sum(msg, dst, num_segments=e.shape[0])
        h = jax.nn.silu(jnp.concatenate([e, agg], axis=-1) @ W1 + b1)
        upd = h @ W2 + b2
        x = e + upd
        mu = jnp.mean(x, axis=-1, keepdims=True)
        var = jnp.mean((x - mu) ** 2, axis=-1, keepdims=True)
        return (x - mu) * jax.lax.rsqrt(var + LN_EPS) * gamma + beta
    edge_index = jnp.stack([src, dst])
    x = _layernorm(x + _L0_gnn_ref(x, edge_index, L0_gnn_W1a, L0_gnn_b1a, L0_gnn_W2a, L0_gnn_b2a, L0_gnn_W1b, L0_gnn_b1b, L0_gnn_W2b, L0_gnn_b2b), axis=-1)
    x = _layernorm(x + _L1_gnn_ref(x, edge_attr_128, src, dst, L1_gnn_Ws, L1_gnn_bs, L1_gnn_Wd, L1_gnn_bd, L1_gnn_Wa, L1_gnn_ba, L1_gnn_Wm, L1_gnn_bm, L1_gnn_W1, L1_gnn_b1, L1_gnn_W2, L1_gnn_b2, L1_gnn_gamma, L1_gnn_beta), axis=-1)
    return x

_drawn_inputs = setup_inputs


def setup_inputs(seed=0):
    import zlib

    import numpy as np

    out = dict(_drawn_inputs(seed))
    spreads = {'L1_gnn_gamma': (1.0, 0.2), 'L1_gnn_beta': (0.0, 0.1)}
    factors = {'edge_attr_128': 8.0,
     'L0_gnn_b1a': 8.0,
     'L0_gnn_b2a': 6.347,
     'L0_gnn_b1b': 4.55,
     'L1_gnn_Ws': 27.347,
     'L1_gnn_bs': 200.0,
     'L1_gnn_Wd': 27.305,
     'L1_gnn_bd': 200.0,
     'L1_gnn_Wa': 8.0,
     'L1_gnn_ba': 200.0,
     'L1_gnn_Wm': 3.974,
     'L1_gnn_bm': 26.852,
     'L1_gnn_b1': 8.0}
    for name, (base, spread) in spreads.items():
        noise = np.random.default_rng([zlib.crc32(name.encode()), seed]).standard_normal(out[name].shape)
        drawn = base * np.exp(spread * noise) if base else spread * noise
        out[name] = jnp.asarray(drawn.astype(out[name].dtype))
    for name, factor in factors.items():
        out[name] = (out[name] * factor).astype(out[name].dtype)
    return out
```

```python
import numpy as np
import concourse.bass as bass
from concourse import mybir
from contextlib import ExitStack

F32 = mybir.dt.float32
BF16 = mybir.dt.bfloat16
I32 = mybir.dt.int32
ALU = mybir.AluOpType
ACT = mybir.ActivationFunctionType
AX = mybir.AxisListType

N, D, E = 50000, 128, 25000
EPS = 1e-5
P = 128
J = 4
GROUP = P * J
GROUPS = -(-N // GROUP)
LAST_BASE = N - GROUP
PAIRS = GROUPS // 2
ROUNDS = (PAIRS - 1) // 2
SLOTS = 4
SPANS = [(0, 43), (43, 86), (86, P)]
K = len(SPANS)
WIDTH = J * 43
BLOCKS = -(-GROUPS * K // P)
ROW = 200
ROWS = E // ROW
SHIFTS = [1 << b for b in range(ROW.bit_length() - 1, -1, -1)]
assert GROUPS % 2 == 0 and PAIRS % 2 == 1 and ROW * ROWS == E and ROWS <= P
assert ROW + P <= 2 * ROW and sum(SHIFTS) + P <= 2 * ROW


def group_base(g):
    return min(g * GROUP, LAST_BASE)


def constants():
    starts = np.full(BLOCKS * P, N, np.float32)
    for g in range(GROUPS):
        for k, (p0, _) in enumerate(SPANS):
            starts[K * g + k] = group_base(g) + J * p0
    rows = np.broadcast_to(starts, (P, BLOCKS * P))
    by_part = starts.reshape(BLOCKS, P).T
    local = (J * np.arange(WIDTH // J)[None, :] + np.arange(J)[:, None]).reshape(-1)
    local = np.broadcast_to(local, (P, WIDTH))
    return np.ascontiguousarray(np.concatenate([rows, by_part, local, np.eye(P)], 1).astype(np.float32))


CONST_COLS = BLOCKS * P + BLOCKS + WIDTH + P


def gnn_kernel(nc, t, out):
    ctx = ExitStack()
    with ctx:
        def sb(name, shape, dt=F32):
            return ctx.enter_context(nc.sbuf_tensor(name, shape, dt))

        def sem(name):
            return ctx.enter_context(nc.semaphore(name))

        def sems(stage, names):
            return {n: sem(f"{stage}_{n}") for n in names.split()}

        def slot_sems(name):
            return [sem(f"{name}{u}") for u in range(SLOTS)]

        x, src, dst, attr = t["x"], t["src"], t["dst"], t["edge_attr_128"]
        h1 = nc.dram_tensor("h1", (N, D), F32, kind="Internal").ap()
        x1 = nc.dram_tensor("x1", (N, D), F32, kind="Internal").ap()

        consts = sb("consts", [P, CONST_COLS])
        o = 0
        starts_row = consts[:, o:o + BLOCKS * P]
        o += BLOCKS * P
        starts_part = consts[:, o:o + BLOCKS]
        o += BLOCKS
        local_node = consts[:, o:o + WIDTH].rearrange("p (j q) -> p j q", j=J)
        o += WIDTH
        ident = consts[:, o:o + P]

        dst_rows = sb("dst_rows", [ROWS, ROW], I32)
        row_last = sb("row_last", [ROWS, 1])
        row_before = sb("row_before", [ROWS, BLOCKS * P])
        ones = sb("ones", [P, 1])
        row_f = sb("row_f", [P, 2 * BLOCKS])
        row_i = sb("row_i", [P, 2 * BLOCKS], I32)
        lists_i = sb("lists_i", [P, BLOCKS, 2, 2 * ROW], I32)
        lists = sb("lists", [P, BLOCKS, 2, 2 * ROW])
        smaller = sb("smaller", [P, BLOCKS, ROW])
        shift = sb("shift", [P, BLOCKS])
        room = sb("room", [P, BLOCKS])
        bit = sb("bit", [P, BLOCKS])
        first = sb("first", [P, BLOCKS])
        moved = sb("moved", [P, 2, 2 * ROW])
        first_edge = sb("first_edge", [1, BLOCKS * P], I32)
        dst_local = sb("dst_local", [P, BLOCKS * P])
        dst_index = sb("dst_index", [P, BLOCKS * P], I32)
        src_index = sb("src_index", [P, BLOCKS * P], I32)

        weights = {n: sb(n, [D, D]) for n in ("W1a", "W2a", "W1b", "W2b", "Ws", "Wd", "Wa", "Wm", "W1x", "W1g", "W2")}
        weight_src = {
            "W1a": t["L0_gnn_W1a"], "W2a": t["L0_gnn_W2a"], "W1b": t["L0_gnn_W1b"], "W2b": t["L0_gnn_W2b"],
            "Ws": t["L1_gnn_Ws"], "Wd": t["L1_gnn_Wd"], "Wa": t["L1_gnn_Wa"], "Wm": t["L1_gnn_Wm"],
            "W1x": t["L1_gnn_W1"][0:D, :], "W1g": t["L1_gnn_W1"][D:2 * D, :], "W2": t["L1_gnn_W2"]}
        cols = ("b1a", "b1b", "bs", "bd", "ba", "bm", "b1")
        col_src = {"b1a": t["L0_gnn_b1a"], "b1b": t["L0_gnn_b1b"], "bs": t["L1_gnn_bs"], "bd": t["L1_gnn_bd"],
                   "ba": t["L1_gnn_ba"], "bm": t["L1_gnn_bm"], "b1": t["L1_gnn_b1"]}
        bias = {n: sb(f"col_{n}", [D, 1]) for n in cols}
        gate_bias = sb("gate_bias", [D, 1])
        rows3 = ("b2a", "b2b", "b2")
        row_src = {"b2a": t["L0_gnn_b2a"], "b2b": t["L0_gnn_b2b"], "b2": t["L1_gnn_b2"]}
        PARTS = 65
        brow = sb("brow", [PARTS, len(rows3), D])
        brest = sb("brest", [PARTS, len(rows3), D])
        bpart = sb("bpart", [PARTS, len(rows3), D], BF16)
        brow_bf = {n: sb(f"row_{n}", [PARTS, J, D], BF16) for n in rows3}
        ones_bf = sb("ones_bf", [PARTS, P], BF16)
        gamma = sb("gamma", [P, J, D])
        beta = sb("beta", [P, J, D])
        minus_half = sb("minus_half", [P, 2 * J])

        xin = [sb(f"xin{u}", [P, J, D]) for u in range(SLOTS)]
        xres = [sb(f"xres{u}", [P, J, D]) for u in range(SLOTS)]
        xsrc = [sb(f"xsrc{u}", [P, K, D]) for u in range(SLOTS)]
        xdst = [sb(f"xdst{u}", [P, K, D]) for u in range(SLOTS)]
        xatt = [sb(f"xatt{u}", [P, K, D]) for u in range(SLOTS)]
        outt = [sb(f"outt{u}", [P, J, D]) for u in range(SLOTS)]
        src_idx = [sb(f"src_idx{u}", [P, K], I32) for u in range(SLOTS)]
        dst_idx = [sb(f"dst_idx{u}", [P, K], I32) for u in range(SLOTS)]
        sel = [sb(f"sel{s}", [P, J, P]) for s in range(2)]
        hT = [sb(f"hT{s}", [P, J, P]) for s in range(2)]
        hid = [sb(f"hid{s}", [P, J, P]) for s in range(2)]
        y = sb("y", [P, SLOTS, J, D])
        norm1 = sb("norm1", [P, SLOTS, J, D])
        y2 = sb("y2", [P, SLOTS, J, D])
        srcT = [sb(f"srcT{s}", [P, K, P]) for s in range(2)]
        dstT = [sb(f"dstT{s}", [P, K, P]) for s in range(2)]
        attT = [sb(f"attT{s}", [P, K, P]) for s in range(2)]
        gate = [sb(f"gate{s}", [P, K, P]) for s in range(2)]
        msgT = [sb(f"msgT{s}", [P, K, P]) for s in range(2)]
        msg = [sb(f"msg{s}", [P, K, P]) for s in range(2)]
        aggT = [sb(f"aggT{s}", [P, J, P]) for s in range(2)]
        sig = [sb(f"sig{s}", [P, J, P]) for s in range(2)]
        LN = [[{part: sb(f"{part}{n}{parity}", [P, 2 * J] + [6] * (part == "stats")) for part in ("stats", "sum", "dif", "var", "rstd", "off")}
               for parity in range(2)] for n in range(2)]

        bank = [[ctx.enter_context(nc.psum_tensor(f"bank{s}{b}", [P, GROUP], F32)) for b in range(4)] for s in range(2)]

        def by_j(b):
            return b[:, :].rearrange("p (j q) -> p j q", j=J)

        def by_k(b):
            return b[:, 0:K * P].rearrange("p (k q) -> p k q", k=K)

        s_const, s_dst, s_wt, s_bcast, s_rows = (sem(n) for n in ("s_const", "s_dst", "s_wt", "s_bcast", "s_rows"))
        v_setup, pe_setup, sp_turn = sem("v_setup"), sem("pe_setup"), sem("pool_turn")
        GIN = "index built agg hT mm1 hid mm2 out yv stats dif var offs rstd"
        layer = [
            {"name": "a", **sems("a", GIN), "in": slot_sems("a_in"), "gathered": slot_sems("a_gathered"), "stored": slot_sems("a_stored"),
             "x": x, "out_rows": h1, "w1": weights["W1a"], "b1": bias["b1a"], "w2": weights["W2a"], "b2": brow_bf["b2a"], "norm": False},
            {"name": "b", **sems("b", GIN), "in": slot_sems("b_in"), "gathered": slot_sems("b_gathered"), "stored": slot_sems("b_stored"),
             "res": slot_sems("b_res"),
             "x": h1, "out_rows": x1, "w1": weights["W1b"], "b1": bias["b1b"], "w2": weights["W2b"], "b2": brow_bf["b2b"], "norm": True},
        ]
        C = {"name": "c", **sems("c", "index built edgeT srcT dstT attT gatemm gate msgT msgtr msg xT xTs aggmm aggT w1 sig hid w2 yv "
                                      "stats1 dif1 var1 rstd1 offs1 norm1 ga gb y2 stats2 dif2 var2 rstd2 offs2 out"),
             "in": slot_sems("c_in"), "gathered": slot_sems("c_gathered"), "att": slot_sems("c_att"), "stored": slot_sems("c_stored")}
        block = ctx.enter_context(nc.Block())

        def pair(i, h):
            return [(i + h // 2, 2 * (h % 2) + s) for s in range(2)]

        def upto(r, u, each=1):
            return (r * SLOTS + u + 1) * each

        def node_rows(dram, r, u):
            base = group_base(SLOTS * r + u) if isinstance(r, int) else r * (SLOTS * GROUP) + u * GROUP
            return dram[bass.ds(base, GROUP), :].rearrange("(p j) f -> p j f", j=J)

        ready = {}

        def rows_stored(eng, L):
            for u in range(SLOTS):
                eng.wait_ge(L["stored"][u], 16 * (ROUNDS + (u < 2)))

        @block.vector
        def _(dve):
            v = nc.vector
            count = [0]

            def step(ins):
                count[0] += 1
                ins.then_inc(v_setup, 1)
                dve.wait_ge(v_setup, count[0])

            step(v.memset(brow[:], 0.0))
            ready["brow"] = count[0]
            dve.wait_ge(s_dst, 16)
            step(v.tensor_copy(row_last[:], dst_rows[:, ROW - 1:ROW]))
            step(v.memset(ones[:], 1.0))
            dve.wait_ge(s_const, 16)
            step(v.tensor_scalar(row_before[:], starts_row[0:ROWS, :], row_last[:, 0:1], None, ALU.is_gt))
            ready["row_before"] = count[0]
            dve.wait_ge(pe_setup, 1)
            step(v.tensor_scalar(row_f[:, 0:BLOCKS], bank[0][0][:, 0:BLOCKS], float(ROWS - 1), None, ALU.min))
            step(v.tensor_scalar(row_f[:, BLOCKS:], bank[0][0][:, 0:BLOCKS], 1.0, float(ROWS - 1), ALU.add, ALU.min))
            step(v.tensor_copy(row_i[:], row_f[:]))
            ready["row_i"] = count[0]
            dve.wait_ge(s_rows, 16 * 4 * BLOCKS)
            step(v.tensor_copy(lists[:], lists_i[:]))
            for b in range(BLOCKS):
                step(v.tensor_scalar(smaller[:, b, :], lists[:, b, 0, 0:ROW], starts_part[:, b:b + 1], None, ALU.is_lt))
            step(v.tensor_reduce(shift[:], smaller[:], AX.X, ALU.add))
            step(v.tensor_scalar(room[:], row_f[:, 0:BLOCKS], float(ROWS - 1), -float(P), ALU.is_ge, ALU.mult))
            step(v.tensor_scalar(room[:], room[:], float(ROW), None, ALU.add))
            step(v.tensor_tensor(shift[:], shift[:], room[:], ALU.min))
            step(v.scalar_tensor_tensor(first[:], row_f[:, 0:BLOCKS], float(ROW), shift[:], ALU.mult, ALU.add))
            for n in SHIFTS:
                step(v.tensor_scalar(bit[:], shift[:], float(n), None, ALU.is_ge))
                width = P + n - 1
                for b in range(BLOCKS):
                    now = lists[:, b, :, 0:width]
                    step(v.tensor_tensor(moved[:, :, 0:width], lists[:, b, :, n:n + width], now, ALU.subtract))
                    step(v.scalar_tensor_tensor(now, moved[:, :, 0:width], bit[:, b:b + 1], now, ALU.mult, ALU.add))
                step(v.scalar_tensor_tensor(shift[:], bit[:], -float(n), shift[:], ALU.mult, ALU.add))
            ready["lists"] = count[0]
            dve.wait_ge(pe_setup, 2)
            flat = bank[0][1][:, 0:BLOCKS * P]
            step(v.tensor_copy(dst_index[:], flat))
            step(v.tensor_tensor(dst_local[:], flat, starts_row, ALU.subtract))
            step(v.tensor_copy(src_index[:], bank[0][2][:, 0:BLOCKS * P]))
            step(v.tensor_copy(first_edge[:], bank[0][3][0:1, 0:BLOCKS * P]))
            ready["tables"] = count[0]
            dve.wait_ge(s_wt, 16 * (len(weights) + len(cols) + 3 * len(rows3) + 2))
            step(v.tensor_tensor(gate_bias[:], bias["bs"][:], bias["bd"][:], ALU.add))
            step(v.tensor_tensor(gate_bias[:], gate_bias[:], bias["ba"][:], ALU.add))
            step(v.memset(ones_bf[:], 1.0))
            step(v.memset(minus_half[:], -0.5))
            for n in rows3:
                step(v.memset(brow_bf[n][:], 0.0))
            for part in range(3):
                rest = brow if part == 0 else brest
                step(v.tensor_copy(bpart[:], rest[:]))
                at = slice(32 * part, 32 * part + 1)
                for k, n in enumerate(rows3):
                    for j in range(J):
                        step(v.tensor_copy(brow_bf[n][at, j, :], bpart[at, k, :]))
                step(v.tensor_tensor(brest[:], rest[:], bpart[:], ALU.subtract))
            ready["all"] = count[0]

            def stage_index(r, u, done, both):
                last = v.tensor_copy(src_idx[u][:], src_index[:, bass.ds((r * SLOTS + u) * K, K)])
                if both:
                    last = v.tensor_copy(dst_idx[u][:], dst_index[:, bass.ds((r * SLOTS + u) * K, K)])
                last.then_inc(done, 1)

            def build(r, u, done):
                for k, (p0, p1) in enumerate(SPANS):
                    at = dst_local[:, bass.ds((r * SLOTS + u) * K + k, 1)]
                    last = v.tensor_scalar(sel[u % 2][:, :, p0:p1], local_node[:, :, 0:p1 - p0], at, None, ALU.is_equal)
                last.then_inc(done, 1)

            def row_stats(values, u, n, done):
                for j in range(J):
                    last = v.bn_stats(LN[n][u // 2]["stats"][:, (u % 2) * J + j, :], values[:, u, j, :])
                last.then_inc(done, 1)

            def moments(q, ln, L, n):
                st = ln["stats"]
                dve.wait_ge(L["stats" + n], 2 * q)
                v.tensor_tensor(ln["sum"][:], st[:, :, 1], st[:, :, 4], ALU.add)
                v.tensor_tensor(ln["dif"][:], st[:, :, 1], st[:, :, 4], ALU.subtract)
                v.scalar_tensor_tensor(ln["var"][:], st[:, :, 2], D * EPS, st[:, :, 5], ALU.add, ALU.add).then_inc(L["dif" + n], 1)
                dve.wait_ge(L["dif" + n], 2 * q - 1)
                v.scalar_tensor_tensor(ln["dif"][:], ln["dif"][:], 0.25, ln["dif"][:], ALU.mult, ALU.mult).then_inc(L["dif" + n], 1)
                dve.wait_ge(L["dif" + n], 2 * q)
                v.scalar_tensor_tensor(ln["var"][:], ln["var"][:], 1.0 / D, ln["dif"][:], ALU.mult, ALU.add).then_inc(L["var" + n], 1)

            def offsets(q, ln, L, n):
                dve.wait_ge(L["rstd" + n], q)
                v.scalar_tensor_tensor(ln["off"][:], ln["sum"][:], -0.5, ln["rstd"][:], ALU.mult, ALU.mult).then_inc(L["offs" + n], 1)

            def gin(L):
                def start(i, h):
                    for r, u in pair(i, h):
                        dve.wait_ge(L["agg"], upto(r, u))
                        v.tensor_copy(hT[u % 2][:], by_j(bank[u % 2][0])).then_inc(L["hT"], 1)
                    if L["norm"] and h > 0:
                        offsets(2 * i + h, LN[0][(h - 1) % 2], L, "")
                    for r, u in pair(i, h + 1):
                        build(r, u, L["built"])
                    for r, u in pair(i, h + 2):
                        stage_index(r, u, L["index"], False)
                    if L["norm"]:
                        for r, u in pair(i, h):
                            dve.wait_ge(L["res"][u], 16 * (r + 1))
                            dve.wait_ge(L["mm2"], upto(r, u))
                            v.scalar_tensor_tensor(y[:, u], by_j(bank[u % 2][2]), 0.0, xres[u][:], ALU.max, ALU.add).then_inc(L["yv"], 1)
                        for r, u in pair(i, h):
                            dve.wait_ge(L["yv"], upto(r, u))
                            row_stats(y, u, 0, L["stats"])
                        moments(2 * i + h + 1, LN[0][h % 2], L, "")

                for r, u in pair(0, 0) + pair(0, 1):
                    stage_index(r, u, L["index"], False)
                for r, u in pair(0, 0):
                    build(r, u, L["built"])
                start(0, 0)
                with dve.Fori(0, ROUNDS) as i:
                    start(i, 1)
                    start(i, 2)
                if L["norm"]:
                    offsets(PAIRS, LN[0][0], L, "")

            def stage_ended(L):
                rows_stored(dve, L)
                dve.wait_ge(L["index"], 2 * (PAIRS + 2))
                dve.wait_ge(L["built"], 2 * (PAIRS + 1))

            gin(layer[0])
            stage_ended(layer[0])
            gin(layer[1])
            stage_ended(layer[1])

            def edges_and_nodes(i, h):
                q = 2 * i + h
                for r, u in pair(i, h):
                    dve.wait_ge(C["edgeT"], upto(r, u))
                    v.tensor_copy(dstT[u % 2][:], by_k(bank[u % 2][1])).then_inc(C["dstT"], 1)
                for r, u in pair(i, h + 2):
                    stage_index(r, u, C["index"], True)
                if h > 0:
                    for r, u in pair(i, h - 1):
                        dve.wait_ge(C["yv"], upto(r, u))
                        row_stats(y, u, 0, C["stats1"])
                    moments(q, LN[0][(h - 1) % 2], C, "1")
                for r, u in pair(i, h):
                    build(r, u, C["built"])
                for r, u in pair(i, h):
                    dve.wait_ge(C["xT"], upto(r, u))
                    v.tensor_copy(hT[u % 2][:], by_j(bank[u % 2][3])).then_inc(C["xTs"], 1)
                if h > 0:
                    offsets(q, LN[0][(h - 1) % 2], C, "1")
                for r, u in pair(i, h):
                    dve.wait_ge(C["gate"], upto(r, u))
                    v.scalar_tensor_tensor(msgT[u % 2][:], by_k(bank[u % 2][0]), bias["bm"][:, 0:1], gate[u % 2][:], ALU.add, ALU.mult).then_inc(C["msgT"], 1)
                for r, u in pair(i, h):
                    dve.wait_ge(C["msgtr"], upto(r, u))
                    v.tensor_copy(msg[u % 2][:], by_k(bank[u % 2][2])).then_inc(C["msg"], 1)
                if h > 0:
                    second_residual(i, h - 1)
                for r, u in pair(i, h):
                    dve.wait_ge(C["sig"], upto(r, u))
                    v.scalar_tensor_tensor(hid[u % 2][:], by_j(bank[u % 2][1]), bias["b1"][:, 0:1], sig[u % 2][:], ALU.add, ALU.mult).then_inc(C["hid"], 1)
                if h > 0:
                    offsets(q, LN[1][(h - 1) % 2], C, "2")
                for r, u in pair(i, h):
                    dve.wait_ge(C["w2"], upto(r, u))
                    v.tensor_tensor(y[:, u], by_j(bank[u % 2][3]), xin[u][:], ALU.add).then_inc(C["yv"], 1)

            def second_residual(i, h):
                q = 2 * i + h + 1
                for r, u in pair(i, h):
                    dve.wait_ge(C["norm1"], upto(r, u))
                    v.tensor_tensor(norm1[:, u], norm1[:, u], gamma[:], ALU.mult).then_inc(C["ga"], 1)
                for r, u in pair(i, h):
                    dve.wait_ge(C["ga"], upto(r, u))
                    v.tensor_tensor(norm1[:, u], norm1[:, u], beta[:], ALU.add).then_inc(C["gb"], 1)
                for r, u in pair(i, h):
                    dve.wait_ge(C["gb"], upto(r, u))
                    v.tensor_tensor(y2[:, u], norm1[:, u], xin[u][:], ALU.add).then_inc(C["y2"], 1)
                for r, u in pair(i, h):
                    dve.wait_ge(C["y2"], upto(r, u))
                    row_stats(y2, u, 1, C["stats2"])
                moments(q, LN[1][h % 2], C, "2")

            for r, u in pair(0, 0) + pair(0, 1):
                stage_index(r, u, C["index"], True)
            edges_and_nodes(0, 0)
            with dve.Fori(0, ROUNDS) as i:
                edges_and_nodes(i, 1)
                edges_and_nodes(i, 2)
            for r, u in pair(ROUNDS, 0):
                dve.wait_ge(C["yv"], upto(r, u))
                row_stats(y, u, 0, C["stats1"])
            moments(PAIRS, LN[0][0], C, "1")
            offsets(PAIRS, LN[0][0], C, "1")
            second_residual(ROUNDS, 0)
            offsets(PAIRS, LN[1][0], C, "2")

        @block.tensor
        def _(pe):
            te = nc.tensor
            pe.wait_ge(v_setup, ready["row_before"])
            for b in range(BLOCKS):
                last = te.matmul(bank[0][0][:, b:b + 1], row_before[:, b * P:(b + 1) * P], ones[0:ROWS, :], start=True, stop=True)
            last.then_inc(pe_setup, 1)
            pe.wait_ge(v_setup, ready["lists"])
            for b in range(BLOCKS):
                at = slice(b * P, (b + 1) * P)
                te.transpose(bank[0][1][:, at], lists[:, b, 0, 0:P], ident)
                te.transpose(bank[0][2][:, at], lists[:, b, 1, 0:P], ident)
                last = te.transpose(bank[0][3][0:1, at], first[:, b:b + 1], ident)
            last.then_inc(pe_setup, 1)
            pe.wait_ge(v_setup, ready["all"])

            def gin(L):
                def steps(i, h):
                    for r, u in pair(i, h):
                        acc = by_j(bank[u % 2][0])
                        pe.wait_ge(L["built"], upto(r, u))
                        pe.wait_ge(L["gathered"][u], 16 * K * (r + 1))
                        for k, (p0, p1) in enumerate(SPANS):
                            te.matmul(acc[:, :, p0:p1], xsrc[u][:, k, :], sel[u % 2][:, :, p0:p1], start=(k == 0), stop=False)
                        pe.wait_ge(L["in"][u], 16 * (r + 1))
                        for j in range(J):
                            last = te.matmul(acc[:, j, :], xin[u][:, j, :], ident, start=False, stop=(j == J - 1), is_transpose=True)
                        last.then_inc(L["agg"], 1)
                    for r, u in pair(i, h):
                        pe.wait_ge(L["hT"], upto(r, u))
                        te.matmul(by_j(bank[u % 2][1]), L["w1"][:], hT[u % 2][:], start=True, stop=True).then_inc(L["mm1"], 1)
                    for r, u in pair(i, h):
                        acc = by_j(bank[u % 2][2])
                        pe.wait_ge(L["hid"], upto(r, u))
                        te.matmul(acc, ones_bf[:], L["b2"][:], start=True, stop=False)
                        for j in range(J):
                            last = te.matmul(acc[:, j, :], hid[u % 2][:, j, :], L["w2"][:], start=False, stop=(j == J - 1))
                        last.then_inc(L["mm2"], 1)
                steps(0, 0)
                with pe.Fori(0, ROUNDS) as i:
                    steps(i, 1)
                    steps(i, 2)
            gin(layer[0])
            rows_stored(pe, layer[0])
            gin(layer[1])
            rows_stored(pe, layer[1])

            def edges_and_nodes(i, h):
                now = pair(i, h)
                for r, u in now:
                    pe.wait_ge(C["gathered"][u], 16 * 2 * K * (r + 1))
                    pe.wait_ge(C["att"][u], 16 * K * (r + 1))
                    for rows, b in ((xsrc, 0), (xdst, 1), (xatt, 2)):
                        for k in range(K):
                            last = te.transpose(by_k(bank[u % 2][b])[:, k, :], rows[u][:, k, :], ident)
                    last.then_inc(C["edgeT"], 1)
                for r, u in now:
                    s = u % 2
                    pe.wait_ge(C["srcT"], upto(r, u))
                    pe.wait_ge(C["dstT"], upto(r, u))
                    pe.wait_ge(C["attT"], upto(r, u))
                    te.matmul(by_k(bank[s][1]), weights["Ws"][:], srcT[s][:], start=True, stop=False)
                    te.matmul(by_k(bank[s][1]), weights["Wd"][:], dstT[s][:], start=False, stop=False)
                    te.matmul(by_k(bank[s][1]), weights["Wa"][:], attT[s][:], start=False, stop=True)
                    te.matmul(by_k(bank[s][0]), weights["Wm"][:], srcT[s][:], start=True, stop=True).then_inc(C["gatemm"], 1)
                for r, u in now:
                    pe.wait_ge(C["in"][u], 16 * (r + 1))
                    if h > 0:
                        pe.wait_ge(C["yv"], upto(r, u) - 2)
                    for j in range(J):
                        last = te.transpose(by_j(bank[u % 2][3])[:, j, :], xin[u][:, j, :], ident)
                    last.then_inc(C["xT"], 1)
                for r, u in now:
                    pe.wait_ge(C["msgT"], upto(r, u))
                    for k in range(K):
                        last = te.transpose(by_k(bank[u % 2][2])[:, k, :], msgT[u % 2][:, k, :], ident)
                    last.then_inc(C["msgtr"], 1)
                for r, u in now:
                    pe.wait_ge(C["xTs"], upto(r, u))
                    te.matmul(by_j(bank[u % 2][1]), weights["W1x"][:], hT[u % 2][:], start=True, stop=False)
                for r, u in now:
                    s = u % 2
                    pe.wait_ge(C["msg"], upto(r, u))
                    pe.wait_ge(C["built"], upto(r, u))
                    for k, (p0, p1) in enumerate(SPANS):
                        last = te.matmul(by_j(bank[s][0])[:, :, p0:p1], msg[s][:, k, :], sel[s][:, :, p0:p1], start=(k == 0), stop=(k == K - 1))
                    last.then_inc(C["aggmm"], 1)
                for r, u in now:
                    pe.wait_ge(C["aggT"], upto(r, u))
                    te.matmul(by_j(bank[u % 2][1]), weights["W1g"][:], aggT[u % 2][:], start=False, stop=True).then_inc(C["w1"], 1)
                for r, u in now:
                    acc = by_j(bank[u % 2][3])
                    pe.wait_ge(C["hid"], upto(r, u))
                    te.matmul(acc, ones_bf[:], brow_bf["b2"][:], start=True, stop=False)
                    for j in range(J):
                        last = te.matmul(acc[:, j, :], hid[u % 2][:, j, :], weights["W2"][:], start=False, stop=(j == J - 1))
                    last.then_inc(C["w2"], 1)
            edges_and_nodes(0, 0)
            with pe.Fori(0, ROUNDS) as i:
                edges_and_nodes(i, 1)
                edges_and_nodes(i, 2)

        @block.scalar
        def _(act):
            a = nc.scalar
            act.wait_ge(v_setup, ready["all"])

            def normed(L, n, dest, values, i, h, then):
                q = 2 * i + h + 1
                ln = LN[n][h % 2]
                act.wait_ge(L[then[0]], q)
                for r, u in pair(i, h):
                    s = u % 2
                    if dest is outt and (r is not 0):
                        act.wait_ge(L["stored"][u], 16 * r)
                    for j in range(J):
                        into = outt[u][:, j, :] if dest is outt else dest[:, u, j, :]
                        c = s * J + j
                        last = a.activation(into, values[:, u, j, :], ACT.Identity, bias=ln["off"][:, c:c + 1], scale=ln["rstd"][:, c:c + 1])
                    last.then_inc(L[then[1]], 1)

            def gin(L):
                def hidden(i, h):
                    for r, u in pair(i, h):
                        act.wait_ge(L["mm1"], upto(r, u))
                        a.activation(hid[u % 2][:], by_j(bank[u % 2][1]), ACT.Relu, bias=L["b1"][:, 0:1]).then_inc(L["hid"], 1)

                def finish(i, h):
                    if L["norm"]:
                        normed(L, 0, outt, y, i, h, ("offs", "out"))
                        return
                    for r, u in pair(i, h):
                        act.wait_ge(L["mm2"], upto(r, u))
                        if r is not 0:
                            act.wait_ge(L["stored"][u], 16 * r)
                        a.activation(outt[u][:], by_j(bank[u % 2][2]), ACT.Relu).then_inc(L["out"], 1)

                def steps(i, h):
                    if L["norm"]:
                        hidden(i, h)
                        finish(i, h - 1)
                    else:
                        finish(i, h - 1)
                        hidden(i, h)
                hidden(0, 0)
                steps(0, 1)
                steps(0, 2)
                with act.Fori(1, ROUNDS) as i:
                    steps(i, 1)
                    steps(i, 2)
                finish(ROUNDS, 0)
            gin(layer[0])
            rows_stored(act, layer[0])
            gin(layer[1])
            rows_stored(act, layer[1])

            def edges_and_nodes(i, h):
                now = pair(i, h)
                for r, u in now:
                    act.wait_ge(C["edgeT"], upto(r, u))
                    a.copy(srcT[u % 2][:], by_k(bank[u % 2][0])).then_inc(C["srcT"], 1)
                    a.copy(attT[u % 2][:], by_k(bank[u % 2][2])).then_inc(C["attT"], 1)
                for r, u in now:
                    act.wait_ge(C["gatemm"], upto(r, u))
                    a.activation(gate[u % 2][:], by_k(bank[u % 2][1]), ACT.Sigmoid, bias=gate_bias[:, 0:1]).then_inc(C["gate"], 1)
                if h > 0:
                    normed(C, 0, norm1, y, i, h - 1, ("offs1", "norm1"))
                for r, u in now:
                    act.wait_ge(C["aggmm"], upto(r, u))
                    a.copy(aggT[u % 2][:], by_j(bank[u % 2][0])).then_inc(C["aggT"], 1)
                for r, u in now:
                    act.wait_ge(C["w1"], upto(r, u))
                    a.activation(sig[u % 2][:], by_j(bank[u % 2][1]), ACT.Sigmoid, bias=bias["b1"][:, 0:1]).then_inc(C["sig"], 1)
                if h > 0:
                    normed(C, 1, outt, y2, i, h - 1, ("offs2", "out"))
            edges_and_nodes(0, 0)
            edges_and_nodes(0, 1)
            edges_and_nodes(0, 2)
            with act.Fori(1, ROUNDS) as i:
                edges_and_nodes(i, 1)
                edges_and_nodes(i, 2)
            normed(C, 0, norm1, y, ROUNDS, 0, ("offs1", "norm1"))
            normed(C, 1, outt, y2, ROUNDS, 0, ("offs2", "out"))

        @block.gpsimd
        def _(pool):
            g = nc.gpsimd

            def by_index(dest, rows, index, done):
                g.indirect_dma_start(dest, None, rows, bass.IndirectOffsetOnAxis(ap=index, axis=0)).then_inc(done, 16)

            pool.wait_ge(v_setup, ready["row_i"])
            for b in range(BLOCKS):
                for half in range(2):
                    at = half * BLOCKS + b
                    for c, edge_list in enumerate((dst, src)):
                        by_index(lists_i[:, b, c, half * ROW:(half + 1) * ROW], edge_list.rearrange("(r c) -> r c", c=ROW), row_i[:, at:at + 1], s_rows)

            def turn(L, r, u):
                pool.wait_ge(L["index"], upto(r, u))
                pool.sem_inc(sp_turn, 1)

            def rstd(q, ln, L, n):
                pool.wait_ge(L["var" + n], q)
                g.tensor_tensor(ln["rstd"][:], ln["var"][:], minus_half[:], ALU.pow).then_inc(L["rstd" + n], 1)

            def gin(L):
                def gather(i, h):
                    for r, u in pair(i, h):
                        turn(L, r, u)
                        for k in range(K):
                            by_index(xsrc[u][:, k, :], L["x"], src_idx[u][:, k:k + 1], L["gathered"][u])

                def steps(i, h, more=True):
                    if more:
                        gather(i, h + 2)
                    if L["norm"]:
                        rstd(2 * i + h + 1, LN[0][h % 2], L, "")
                gather(0, 0)
                gather(0, 1)
                steps(0, 0)
                with pool.Fori(0, ROUNDS - 1) as i:
                    steps(i, 1)
                    steps(i, 2)
                steps(ROUNDS - 1, 1, False)
                steps(ROUNDS - 1, 2, False)
            gin(layer[0])
            rows_stored(pool, layer[0])
            gin(layer[1])
            rows_stored(pool, layer[1])

            def gather_one(r, u):
                turn(C, r, u)
                for rows, idx in ((xsrc, src_idx), (xdst, dst_idx)):
                    for k in range(K):
                        by_index(rows[u][:, k, :], x1, idx[u][:, k:k + 1], C["gathered"][u])

            def steps(i, h, more=True):
                q = 2 * i + h
                ahead = pair(i, h + 2)
                if more:
                    gather_one(*ahead[0])
                if h > 0:
                    rstd(q, LN[0][(h - 1) % 2], C, "1")
                if more:
                    gather_one(*ahead[1])
                if h > 0:
                    rstd(q, LN[1][(h - 1) % 2], C, "2")
            for r, u in pair(0, 0) + pair(0, 1):
                gather_one(r, u)
            steps(0, 0)
            with pool.Fori(0, ROUNDS - 1) as i:
                steps(i, 1)
                steps(i, 2)
            steps(ROUNDS - 1, 1, False)
            steps(ROUNDS - 1, 2, False)
            rstd(PAIRS, LN[0][0], C, "1")
            rstd(PAIRS, LN[1][0], C, "2")

        @block.sync
        def _(sp):
            sp.dma_start(dst_rows[:], dst.rearrange("(r c) -> r c", c=ROW)).then_inc(s_dst, 16)
            sp.dma_start(consts[:], t["constants"]).then_inc(s_const, 16)
            for n in weights:
                sp.dma_start(weights[n][:], weight_src[n]).then_inc(s_wt, 16)
            for n in cols:
                sp.dma_start(bias[n][:], col_src[n].rearrange("(f o) -> f o", o=1)).then_inc(s_wt, 16)
            sp.wait_ge(v_setup, ready["brow"])
            for k, n in enumerate(rows3):
                for p in range(0, PARTS, 32):
                    sp.dma_start(brow[p:p + 1, k, :], row_src[n].rearrange("(o f) -> o f", o=1)).then_inc(s_wt, 16)
            for tile, vec in ((gamma, t["L1_gnn_gamma"]), (beta, t["L1_gnn_beta"])):
                sp.dma_start(tile[:], vec.partition_broadcast(P).rearrange("p (o f) -> p o f", o=1).to_broadcast([P, J, D])).then_inc(s_wt, 16)

            def stage(L, load, target, used):
                def store(i, h):
                    for r, u in pair(i, h):
                        sp.wait_ge(L["out"], upto(r, u))
                        sp.dma_start(node_rows(target, r, u), outt[u][:]).then_inc(L["stored"][u], 16)

                def steps(i, h, more=True):
                    if more:
                        for r, u in pair(i, h + 2):
                            sp.wait_ge(used, upto(r - 1, u))
                            load(r, u)
                    if h > 0:
                        store(i, h - 1)
                for r, u in pair(0, 0) + pair(0, 1):
                    load(r, u)
                steps(0, 0)
                with sp.Fori(0, ROUNDS - 2) as i:
                    steps(i, 1)
                    steps(i, 2)
                steps(ROUNDS - 2, 1)
                steps(ROUNDS - 2, 2)
                steps(ROUNDS - 1, 1, False)
                steps(ROUNDS - 1, 2, False)
                (r, u), (r2, u2) = pair(ROUNDS, 0)
                sp.wait_ge(L["out"], upto(r, u))
                sp.dma_start(node_rows(target, r, u), outt[u][:]).then_inc(L["stored"][u], 16)
                for w in range(SLOTS):
                    sp.wait_ge(L["stored"][w], 16 * (ROUNDS + (w < 1)))
                sp.wait_ge(L["out"], upto(r2, u2))
                sp.dma_start(node_rows(target, r2, u2), outt[u2][:]).then_inc(L["stored"][u2], 16)
                sp.wait_ge(L["stored"][u2], 16 * (ROUNDS + 1))

            def load_a(r, u):
                sp.dma_start(xin[u][:], node_rows(x, r, u)).then_inc(layer[0]["in"][u], 16)

            def load_b(r, u):
                sp.dma_start(xin[u][:], node_rows(h1, r, u)).then_inc(layer[1]["in"][u], 16)
                sp.dma_start(xres[u][:], node_rows(x, r, u)).then_inc(layer[1]["res"][u], 16)

            def load_c(r, u):
                sp.dma_start(xin[u][:], node_rows(x1, r, u)).then_inc(C["in"][u], 16)
                for k in range(K):
                    at = sp.value_load(first_edge[0:1, bass.ds((r * SLOTS + u) * K + k, 1)], min_val=0, max_val=E - P)
                    sp.dma_start(xatt[u][:, k, :], attr[bass.ds(at, P), :]).then_inc(C["att"][u], 16)

            stage(layer[0], load_a, h1, layer[0]["agg"])
            stage(layer[1], load_b, x1, layer[1]["yv"])
            sp.wait_ge(v_setup, ready["tables"])
            stage(C, load_c, out, C["y2"])


_INS = ['x', 'src', 'dst', 'edge_attr_128',
        'L0_gnn_W1a', 'L0_gnn_b1a', 'L0_gnn_W2a', 'L0_gnn_b2a', 'L0_gnn_W1b', 'L0_gnn_b1b', 'L0_gnn_W2b', 'L0_gnn_b2b',
        'L1_gnn_Ws', 'L1_gnn_bs', 'L1_gnn_Wd', 'L1_gnn_bd', 'L1_gnn_Wa', 'L1_gnn_ba', 'L1_gnn_Wm', 'L1_gnn_bm',
        'L1_gnn_W1', 'L1_gnn_b1', 'L1_gnn_W2', 'L1_gnn_b2', 'L1_gnn_gamma', 'L1_gnn_beta']


def kernel(**inputs):
    import numpy as _np
    import concourse.bacc as _bacc
    from concourse import mybir as _mybir
    from concourse.bass_utils import run_bass_kernel_spmd as _run

    nc = _bacc.Bacc("TRN2", target_bir_lowering=False, num_devices=1)
    arrays, args = {}, {}
    given = {name: _np.ascontiguousarray(inputs[name]) for name in _INS}
    given["constants"] = constants()
    for name, a in given.items():
        arrays[f"in_{name}"] = a
        args[name] = nc.dram_tensor(f"in_{name}", a.shape, _mybir.dt.from_np(a.dtype), kind="ExternalInput").ap()
    out = nc.dram_tensor("out_0_dram", (N, D), F32, kind="ExternalOutput").ap()
    gnn_kernel(nc, args, out)
    r = _run(nc, [arrays], core_ids=[0])
    return r.results[0]["out_0_dram"]
```

```python
import numpy as np
import concourse.bass as bass
from concourse import mybir
from contextlib import ExitStack

F32 = mybir.dt.float32
BF16 = mybir.dt.bfloat16
I32 = mybir.dt.int32
ALU = mybir.AluOpType
ACT = mybir.ActivationFunctionType
AX = mybir.AxisListType

N, D, E = 50000, 128, 25000
EPS = 1e-5
NEWTON = 3
LINKS = 2 + 3 * NEWTON + 1
P = 128
J = 4
GROUP = P * J
GROUPS = -(-N // GROUP)
LAST_BASE = N - GROUP
BODY = 8
ROUNDS = GROUPS // BODY
SLOTS = 4
SPANS = [(0, 43), (43, 86), (86, P)]
K = len(SPANS)
WIDTH = J * 43
BLOCKS = -(-GROUPS * K // P)
ROW = 200
ROWS = E // ROW
SHIFTS = [1 << b for b in range(ROW.bit_length() - 1, -1, -1)]
assert GROUPS % 2 == 0 and ROW * ROWS == E and ROWS <= P
assert ROW + P <= 2 * ROW and sum(SHIFTS) + P <= 2 * ROW


def group_base(g):
    return min(g * GROUP, LAST_BASE)


def constants():
    starts = np.full(BLOCKS * P, N, np.float32)
    for g in range(GROUPS):
        for k, (p0, _) in enumerate(SPANS):
            starts[K * g + k] = group_base(g) + J * p0
    rows = np.broadcast_to(starts, (P, BLOCKS * P))
    by_part = starts.reshape(BLOCKS, P).T
    local = (J * np.arange(WIDTH // J)[None, :] + np.arange(J)[:, None]).reshape(-1)
    local = np.broadcast_to(local, (P, WIDTH))
    return np.ascontiguousarray(np.concatenate([rows, by_part, local, np.eye(P)], 1).astype(np.float32))


CONST_COLS = BLOCKS * P + BLOCKS + WIDTH + P


def gnn_kernel(nc, t, out):
    ctx = ExitStack()
    with ctx:
        def sb(name, shape, dt=F32):
            return ctx.enter_context(nc.sbuf_tensor(name, shape, dt))

        def sem(name):
            return ctx.enter_context(nc.semaphore(name))

        def sems(stage, names):
            return {n: sem(f"{stage}_{n}") for n in names.split()}

        def slot_sems(name, slots=SLOTS):
            return [sem(f"{name}{u}") for u in range(slots)]

        x, src, dst, attr = t["x"], t["src"], t["dst"], t["edge_attr_128"]
        h1 = nc.dram_tensor("h1", (N, D), F32, kind="Internal").ap()
        x1 = nc.dram_tensor("x1", (N, D), F32, kind="Internal").ap()

        consts = sb("consts", [P, CONST_COLS])
        o = 0
        starts_row = consts[:, o:o + BLOCKS * P]
        o += BLOCKS * P
        starts_part = consts[:, o:o + BLOCKS]
        o += BLOCKS
        local_node = consts[:, o:o + WIDTH].rearrange("p (j q) -> p j q", j=J)
        o += WIDTH
        ident = consts[:, o:o + P]

        dst_rows = sb("dst_rows", [ROWS, ROW], I32)
        row_last = sb("row_last", [ROWS, 1])
        row_before = sb("row_before", [ROWS, BLOCKS * P])
        ones = sb("ones", [P, 1])
        row_f = sb("row_f", [P, 2 * BLOCKS])
        row_i = sb("row_i", [P, 2 * BLOCKS], I32)
        lists_i = sb("lists_i", [P, BLOCKS, 2, 2 * ROW], I32)
        lists = sb("lists", [P, BLOCKS, 2, 2 * ROW])
        smaller = sb("smaller", [P, BLOCKS, ROW])
        shift = sb("shift", [P, BLOCKS])
        room = sb("room", [P, BLOCKS])
        bit = sb("bit", [P, BLOCKS])
        first = sb("first", [P, BLOCKS])
        moved = sb("moved", [P, 2, 2 * ROW])
        first_edge = sb("first_edge", [1, BLOCKS * P], I32)
        dst_local = sb("dst_local", [P, BLOCKS * P])
        dst_index = sb("dst_index", [P, BLOCKS * P], I32)
        src_index = sb("src_index", [P, BLOCKS * P], I32)

        weights = {n: sb(n, [D, D]) for n in ("W1a", "W2a", "W1b", "W2b", "Ws", "Wd", "Wa", "Wm", "W1x", "W1g", "W2")}
        weight_src = {
            "W1a": t["L0_gnn_W1a"], "W2a": t["L0_gnn_W2a"], "W1b": t["L0_gnn_W1b"], "W2b": t["L0_gnn_W2b"],
            "Ws": t["L1_gnn_Ws"], "Wd": t["L1_gnn_Wd"], "Wa": t["L1_gnn_Wa"], "Wm": t["L1_gnn_Wm"],
            "W1x": t["L1_gnn_W1"][0:D, :], "W1g": t["L1_gnn_W1"][D:2 * D, :], "W2": t["L1_gnn_W2"]}
        cols = ("b1a", "b1b", "bs", "bd", "ba", "bm", "b1")
        col_src = {"b1a": t["L0_gnn_b1a"], "b1b": t["L0_gnn_b1b"], "bs": t["L1_gnn_bs"], "bd": t["L1_gnn_bd"],
                   "ba": t["L1_gnn_ba"], "bm": t["L1_gnn_bm"], "b1": t["L1_gnn_b1"]}
        bias = {n: sb(f"col_{n}", [D, 1]) for n in cols}
        gate_bias = sb("gate_bias", [D, 1])
        rows3 = ("b2a", "b2b", "b2")
        row_src = {"b2a": t["L0_gnn_b2a"], "b2b": t["L0_gnn_b2b"], "b2": t["L1_gnn_b2"]}
        PARTS = 65
        brow = sb("brow", [PARTS, len(rows3), D])
        brest = sb("brest", [PARTS, len(rows3), D])
        bpart = sb("bpart", [PARTS, len(rows3), D], BF16)
        brow_bf = {n: sb(f"row_{n}", [PARTS, J, D], BF16) for n in rows3}
        ones_bf = sb("ones_bf", [PARTS, P], BF16)
        gamma = sb("gamma", [P, J, D])
        beta = sb("beta", [P, J, D])
        
        xin = [sb(f"xin{u}", [P, J, D]) for u in range(BODY)]
        xres = [sb(f"xres{u}", [P, J, D]) for u in range(BODY)]
        xsrc = [sb(f"xsrc{u}", [P, K, D]) for u in range(SLOTS)]
        xdst = [sb(f"xdst{u}", [P, K, D]) for u in range(SLOTS)]
        xatt = [sb(f"xatt{u}", [P, K, D]) for u in range(SLOTS)]
        outt = [sb(f"outt{u}", [P, J, D]) for u in range(SLOTS)]
        src_idx = [sb(f"src_idx{u}", [P, K], I32) for u in range(SLOTS)]
        dst_idx = [sb(f"dst_idx{u}", [P, K], I32) for u in range(SLOTS)]
        sel = [sb(f"sel{s}", [P, J, P]) for s in range(2)]
        hT = [sb(f"hT{s}", [P, J, P]) for s in range(2)]
        hid = [sb(f"hid{s}", [P, J, P]) for s in range(2)]
        y = sb("y", [P, SLOTS, J, D])
        norm1 = sb("norm1", [P, SLOTS, J, D])
        y2 = sb("y2", [P, SLOTS, J, D])
        srcT = sb("srcT", [P, K, P])
        dstT = sb("dstT", [P, K, P])
        attT = sb("attT", [P, K, P])
        gate = sb("gate", [P, K, P])
        msgT = sb("msgT", [P, K, P])
        msg = sb("msg", [P, K, P])
        aggT = sb("aggT", [P, J, P])
        sig = sb("sig", [P, J, P])
        PAIR = 2 * J
        LN = [{"stats": sb(f"stats{p}", [P, 2, PAIR, 6]), "rest": sb(f"rest{p}", [P, 2 * PAIR]), "half": sb(f"half{p}", [P, 2 * PAIR], I32),
               **{part: sb(f"{part}{p}", [P, 2 * PAIR]) for part in ("sum", "dif", "var", "rstd", "off")}} for p in range(2)]

        banks = [ctx.enter_context(nc.psum_tensor(f"bank{b}", [P, GROUP], F32)) for b in range(8)]

        def by_j(b):
            return b[:, :].rearrange("p (j q) -> p j q", j=J)

        def by_k(b):
            return b[:, 0:K * P].rearrange("p (k q) -> p k q", k=K)

        s_const, s_dst, s_wt, s_bcast, s_rows = (sem(n) for n in ("s_const", "s_dst", "s_wt", "s_bcast", "s_rows"))
        v_setup, pe_setup, pool_turn = sem("v_setup"), sem("pe_setup"), sem("pool_turn")

        def layer_sems(name, names):
            return {"name": name, **sems(name, names), "in": slot_sems(f"{name}_in", BODY),
                    "gathered": slot_sems(f"{name}_gathered"), "stored": slot_sems(f"{name}_stored")}

        GIN = "index built agg hT mm1 hid mm2 out"
        A = {**layer_sems("a", GIN), "x": x, "w1": weights["W1a"], "b1": bias["b1a"], "w2": weights["W2a"], "b2": brow_bf["b2a"], "norm": False}
        B = {**layer_sems("b", GIN + " y stats dif var chain"), "res": slot_sems("b_res", BODY),
             "x": h1, "w1": weights["W1b"], "b1": bias["b1b"], "w2": weights["W2b"], "b2": brow_bf["b2b"], "norm": True}
        C = {**layer_sems("c", "index built edgeT srcT dstT attT gatemm gate msgT msgtr msg xT xTs aggmm aggT w1 sig hid w2 y "
                          "stats dif var norm ga gb y2 stats2 dif2 var2 chain out"),
             "att": slot_sems("c_att")}
        block = ctx.enter_context(nc.Block())

        def group_at(r, u, lag):
            n = u - lag
            group = (r + n // BODY, n % BODY)
            if isinstance(r, int) and not 0 <= number(*group) < GROUPS:
                return None
            return group

        def number(r, u):
            return r * BODY + u

        def upto(r, u):
            return r * BODY + u + 1

        def slot_uses(r, u):
            return r * (BODY // SLOTS) + u // SLOTS + 1

        def pairs_upto(r, u):
            return r * (BODY // 2) + (u + 1) // 2

        def ln_of(u):
            return LN[u // 2 % 2]

        def run(eng, step, lead, lag, exact=False):
            first = -(-lag // BODY) if lag > BODY else 1
            for g in range(-lead, first * BODY):
                step(g // BODY, g % BODY)
            last = ROUNDS - (1 if exact else 0)
            with eng.Fori(first, last) as r:
                for u in range(BODY):
                    step(r, u)
            for g in range(last * BODY, GROUPS + lag):
                step(g // BODY, g % BODY)

        def node_rows(dram, r, u):
            base = group_base(number(r, u)) if isinstance(r, int) else r * (BODY * GROUP) + u * GROUP
            return dram[bass.ds(base, GROUP), :].rearrange("(p j) f -> p j f", j=J)

        def rows_stored(eng, L):
            for s in range(SLOTS):
                eng.wait_ge(L["stored"][s], 16 * len(range(s, GROUPS, SLOTS)))

        ready = {}

        @block.vector
        def _(dve):
            v = nc.vector
            count = [0]

            def step(ins):
                count[0] += 1
                ins.then_inc(v_setup, 1)
                dve.wait_ge(v_setup, count[0])

            step(v.memset(brow[:], 0.0))
            ready["brow"] = count[0]
            dve.wait_ge(s_dst, 16)
            step(v.tensor_copy(row_last[:], dst_rows[:, ROW - 1:ROW]))
            step(v.memset(ones[:], 1.0))
            dve.wait_ge(s_const, 16)
            step(v.tensor_scalar(row_before[:], starts_row[0:ROWS, :], row_last[:, 0:1], None, ALU.is_gt))
            ready["row_before"] = count[0]
            dve.wait_ge(pe_setup, 1)
            step(v.tensor_scalar(row_f[:, 0:BLOCKS], banks[0][:, 0:BLOCKS], float(ROWS - 1), None, ALU.min))
            step(v.tensor_scalar(row_f[:, BLOCKS:], banks[0][:, 0:BLOCKS], 1.0, float(ROWS - 1), ALU.add, ALU.min))
            step(v.tensor_copy(row_i[:], row_f[:]))
            ready["row_i"] = count[0]
            dve.wait_ge(s_rows, 16 * 4 * BLOCKS)
            step(v.tensor_copy(lists[:], lists_i[:]))
            for b in range(BLOCKS):
                step(v.tensor_scalar(smaller[:, b, :], lists[:, b, 0, 0:ROW], starts_part[:, b:b + 1], None, ALU.is_lt))
            step(v.tensor_reduce(shift[:], smaller[:], AX.X, ALU.add))
            step(v.tensor_scalar(room[:], row_f[:, 0:BLOCKS], float(ROWS - 1), -float(P), ALU.is_ge, ALU.mult))
            step(v.tensor_scalar(room[:], room[:], float(ROW), None, ALU.add))
            step(v.tensor_tensor(shift[:], shift[:], room[:], ALU.min))
            step(v.scalar_tensor_tensor(first[:], row_f[:, 0:BLOCKS], float(ROW), shift[:], ALU.mult, ALU.add))
            for n in SHIFTS:
                step(v.tensor_scalar(bit[:], shift[:], float(n), None, ALU.is_ge))
                width = P + n - 1
                for b in range(BLOCKS):
                    now = lists[:, b, :, 0:width]
                    step(v.tensor_tensor(moved[:, :, 0:width], lists[:, b, :, n:n + width], now, ALU.subtract))
                    step(v.scalar_tensor_tensor(now, moved[:, :, 0:width], bit[:, b:b + 1], now, ALU.mult, ALU.add))
                step(v.scalar_tensor_tensor(shift[:], bit[:], -float(n), shift[:], ALU.mult, ALU.add))
            ready["lists"] = count[0]
            dve.wait_ge(pe_setup, 2)
            flat = banks[1][:, 0:BLOCKS * P]
            step(v.tensor_copy(dst_index[:], flat))
            step(v.tensor_tensor(dst_local[:], flat, starts_row, ALU.subtract))
            step(v.tensor_copy(src_index[:], banks[2][:, 0:BLOCKS * P]))
            step(v.tensor_copy(first_edge[:], banks[3][0:1, 0:BLOCKS * P]))
            ready["tables"] = count[0]
            dve.wait_ge(s_wt, 16 * (len(weights) + len(cols) + 3 * len(rows3) + 2))
            step(v.tensor_tensor(gate_bias[:], bias["bs"][:], bias["bd"][:], ALU.add))
            step(v.tensor_tensor(gate_bias[:], gate_bias[:], bias["ba"][:], ALU.add))
            step(v.memset(ones_bf[:], 1.0))
            for n in rows3:
                step(v.memset(brow_bf[n][:], 0.0))
            for part in range(3):
                rest = brow if part == 0 else brest
                step(v.tensor_copy(bpart[:], rest[:]))
                at = slice(32 * part, 32 * part + 1)
                for k, n in enumerate(rows3):
                    for j in range(J):
                        step(v.tensor_copy(brow_bf[n][at, j, :], bpart[at, k, :]))
                step(v.tensor_tensor(brest[:], rest[:], bpart[:], ALU.subtract))
            for p in range(2):
                step(v.memset(LN[p]["var"][:], 1.0))
                step(v.memset(LN[p]["sum"][:], 0.0))
            ready["all"] = count[0]

            def stage_index(group, L):
                if group is None:
                    return
                r, u = group
                last = v.tensor_copy(src_idx[u % SLOTS][:], src_index[:, bass.ds(number(r, u) * K, K)])
                if L is C:
                    last = v.tensor_copy(dst_idx[u % SLOTS][:], dst_index[:, bass.ds(number(r, u) * K, K)])
                last.then_inc(L["index"], 1)

            def build(group, L, only=None):
                if group is None:
                    return
                r, u = group
                for k, (p0, p1) in enumerate(SPANS):
                    if only is not None and k != only:
                        continue
                    goes_to = dst_local[:, bass.ds(number(r, u) * K + k, 1)]
                    last = v.tensor_scalar(sel[u % 2][:, :, p0:p1], local_node[:, :, 0:p1 - p0], goes_to, None, ALU.is_equal)
                if only in (None, K - 1):
                    last.then_inc(L["built"], 1)

            def row_stats(values, u, n, done):
                for j in range(J):
                    last = v.bn_stats(ln_of(u)["stats"][:, n, (u % 2) * J + j, :], values[:, u % SLOTS, j, :])
                last.then_inc(done, 1)

            def moments(group, n, L, tag):
                if group is None:
                    return
                ln, pairs = ln_of(group[1]), pairs_upto(*group)
                st = ln["stats"][:, n]
                total, dif, var = (ln[part][:, n * PAIR:(n + 1) * PAIR] for part in ("sum", "dif", "var"))
                dve.wait_ge(L["stats" + tag], upto(*group))
                v.tensor_tensor(total, st[:, :, 1], st[:, :, 4], ALU.add)
                v.tensor_tensor(dif, st[:, :, 1], st[:, :, 4], ALU.subtract)
                v.scalar_tensor_tensor(var, st[:, :, 2], D * EPS, st[:, :, 5], ALU.add, ALU.add).then_inc(L["dif" + tag], 1)
                dve.wait_ge(L["dif" + tag], 2 * pairs - 1)
                v.scalar_tensor_tensor(dif, dif, 0.25, dif, ALU.mult, ALU.mult).then_inc(L["dif" + tag], 1)
                dve.wait_ge(L["dif" + tag], 2 * pairs)
                v.scalar_tensor_tensor(var, var, 1.0 / D, dif, ALU.mult, ALU.add).then_inc(L["var" + tag], 1)

            class Scales:

                def __init__(self, group, chain_no, L, cols, var_done):
                    self.group, self.no, self.L, self.cols, self.at, self.var_done = group, chain_no, L, cols, 0, var_done

                def go(self, links=1):
                    if self.group is None:
                        return
                    ln = ln_of(self.group[1])
                    c = slice(0, self.cols)
                    for _ in range(links):
                        n, self.at = self.at, self.at + 1
                        if n == 0:
                            for name, value in self.var_done:
                                dve.wait_ge(self.L[name], value)
                        else:
                            dve.wait_ge(self.L["chain"], self.no * LINKS - (LINKS - n))
                        if n == 0:
                            ins = v.tensor_single_scalar(ln["half"][:, c], ln["var"][:, c].bitcast(I32), 1, ALU.logical_shift_right)
                        elif n == 1:
                            ins = v.tensor_scalar(ln["rstd"][:, c].bitcast(I32), ln["half"][:, c], -1.0, float(0x5F3759DF), ALU.mult, ALU.add)
                        elif n == LINKS - 1:
                            ins = v.scalar_tensor_tensor(ln["off"][:, c], ln["sum"][:, c], -0.5, ln["rstd"][:, c], ALU.mult, ALU.mult)
                        elif n % 3 == 2:
                            ins = v.tensor_tensor(ln["rest"][:, c], ln["rstd"][:, c], ln["rstd"][:, c], ALU.mult)
                        elif n % 3 == 0:
                            ins = v.scalar_tensor_tensor(ln["rest"][:, c], ln["rest"][:, c], -0.5, ln["var"][:, c], ALU.mult, ALU.mult)
                        else:
                            ins = v.scalar_tensor_tensor(ln["rstd"][:, c], ln["rest"][:, c], 1.5, ln["rstd"][:, c], ALU.add, ALU.mult)
                        ins.then_inc(self.L["chain"], 1)

                def end(self):
                    self.go(LINKS - self.at)

            def stage_ended(L, indexed, built):
                rows_stored(dve, L)
                dve.wait_ge(L["index"], indexed)
                dve.wait_ge(L["built"], built)

            def gin(L):
                def step(r, u):
                    if not L["norm"]:
                        if now := group_at(r, u, 0):
                            dve.wait_ge(L["agg"], upto(*now))
                            v.tensor_copy(hT[u % 2][:], by_j(banks[u % 2])).then_inc(L["hT"], 1)
                        stage_index(group_at(r, u, -SLOTS), L)
                        build(group_at(r, u, -1), L)
                        return
                    ended = group_at(r, u, 3) if u % 2 == 0 else None
                    scales = Scales(ended, pairs_upto(*ended) if ended else 0, L, PAIR, [("var", pairs_upto(*ended))] if ended else [])
                    if now := group_at(r, u, 0):
                        dve.wait_ge(L["agg"], upto(*now))
                    stage_index(group_at(r, u, -SLOTS), L)
                    scales.go(3)
                    nxt = group_at(r, u, -1)
                    for k in range(K):
                        build(nxt, L, k)
                        scales.go(2)
                    last = group_at(r, u, 2)
                    if last:
                        lr, lu = last
                        dve.wait_ge(L["res"][lu], 16 * (lr + 1))
                        dve.wait_ge(L["mm2"], upto(lr, lu))
                        v.scalar_tensor_tensor(y[:, lu % SLOTS], by_j(banks[4 + lu % 2]), 0.0, xres[lu][:], ALU.max, ALU.add).then_inc(L["y"], 1)
                    scales.end()
                    if last:
                        dve.wait_ge(L["y"], upto(lr, lu))
                        row_stats(y, lu, 0, L["stats"])
                    if u % 2 == 1:
                        moments(group_at(r, u, 2), 0, L, "")
                for g in range(SLOTS):
                    stage_index((0, g), L)
                build((0, 0), L)
                run(dve, step, 0, 4 if L["norm"] else 0)

            gin(A)
            stage_ended(A, GROUPS + 2, GROUPS)
            gin(B)
            stage_ended(B, GROUPS + 2, GROUPS)

            def step_c(r, u):
                now, nxt, last, old = group_at(r, u, 0), group_at(r, u, -1), group_at(r, u, 1), group_at(r, u, 5)
                first_pair, second_pair = (group_at(r, u, lag) if u % 2 == 1 else None for lag in (2, 6))
                waits = ([("var", pairs_upto(*first_pair))] if first_pair else []) + ([("var2", pairs_upto(*second_pair))] if second_pair else [])
                either = first_pair or second_pair
                scales = Scales(either, (r * BODY + u - 1) // 2 if isinstance(r, int) else r * (BODY // 2) + (u - 1) // 2, C, 2 * PAIR, waits)
                stage_index(group_at(r, u, -SLOTS), C)
                if now:
                    dve.wait_ge(C["msgtr"], upto(*now))
                    v.tensor_copy(msg[:], by_k(banks[3])).then_inc(C["msg"], 1)
                scales.go()
                if last:
                    dve.wait_ge(C["sig"], upto(*last))
                    v.scalar_tensor_tensor(hid[0][:], by_j(banks[6]), bias["b1"][:, 0:1], sig[:], ALU.add, ALU.mult).then_inc(C["hid"], 1)
                scales.go()
                for k in range(K):
                    build(nxt, C, k)
                    scales.go(2)
                if old:
                    ou = old[1] % SLOTS
                    dve.wait_ge(C["norm"], upto(*old))
                    v.tensor_tensor(norm1[:, ou], norm1[:, ou], gamma[:], ALU.mult).then_inc(C["ga"], 1)
                scales.go(2)
                if last:
                    lu = last[1]
                    dve.wait_ge(C["w2"], upto(*last))
                    v.tensor_tensor(y[:, lu % SLOTS], by_j(banks[7]), xin[lu][:], ALU.add).then_inc(C["y"], 1)
                scales.end()
                if old:
                    dve.wait_ge(C["ga"], upto(*old))
                    v.tensor_tensor(norm1[:, ou], norm1[:, ou], beta[:], ALU.add).then_inc(C["gb"], 1)
                if last:
                    dve.wait_ge(C["y"], upto(*last))
                    row_stats(y, lu, 0, C["stats"])
                if old:
                    dve.wait_ge(C["gb"], upto(*old))
                    v.tensor_tensor(y2[:, ou], norm1[:, ou], xin[old[1]][:], ALU.add).then_inc(C["y2"], 1)
                if nxt:
                    dve.wait_ge(C["gate"], upto(*nxt))
                    v.scalar_tensor_tensor(msgT[:], by_k(banks[0]), bias["bm"][:, 0:1], gate[:], ALU.add, ALU.mult).then_inc(C["msgT"], 1)
                if u % 2 == 0:
                    moments(last, 0, C, "")
                if old:
                    dve.wait_ge(C["y2"], upto(*old))
                    row_stats(y2, old[1], 1, C["stats2"])
                if u % 2 == 0:
                    moments(old, 1, C, "2")

            for g in range(SLOTS - 1):
                stage_index((0, g), C)
            run(dve, step_c, 1, 6)

        @block.tensor
        def _(pe):
            te = nc.tensor
            pe.wait_ge(v_setup, ready["row_before"])
            for b in range(BLOCKS):
                last = te.matmul(banks[0][:, b:b + 1], row_before[:, b * P:(b + 1) * P], ones[0:ROWS, :], start=True, stop=True)
            last.then_inc(pe_setup, 1)
            pe.wait_ge(v_setup, ready["lists"])
            for b in range(BLOCKS):
                at = slice(b * P, (b + 1) * P)
                te.transpose(banks[1][:, at], lists[:, b, 0, 0:P], ident)
                te.transpose(banks[2][:, at], lists[:, b, 1, 0:P], ident)
                last = te.transpose(banks[3][0:1, at], first[:, b:b + 1], ident)
            last.then_inc(pe_setup, 1)
            pe.wait_ge(v_setup, ready["all"])

            def gin(L):
                def step(r, u):
                    if now := group_at(r, u, 0):
                        acc = by_j(banks[u % 2])
                        pe.wait_ge(L["built"], upto(*now))
                        pe.wait_ge(L["gathered"][u % SLOTS], slot_uses(*now) * (16 * K))
                        for k, (p0, p1) in enumerate(SPANS):
                            te.matmul(acc[:, :, p0:p1], xsrc[u % SLOTS][:, k, :], sel[u % 2][:, :, p0:p1], start=(k == 0), stop=False)
                        pe.wait_ge(L["in"][u], 16 * (now[0] + 1))
                        for j in range(J):
                            last = te.matmul(acc[:, j, :], xin[u][:, j, :], ident, start=False, stop=(j == J - 1), is_transpose=True)
                        last.then_inc(L["agg"], 1)
                    if group := group_at(r, u, 1):
                        s = group[1] % 2
                        pe.wait_ge(L["hT"], upto(*group))
                        te.matmul(by_j(banks[2 + s]), L["w1"][:], hT[s][:], start=True, stop=True).then_inc(L["mm1"], 1)
                    if group := group_at(r, u, 2):
                        s = group[1] % 2
                        acc = by_j(banks[4 + s])
                        pe.wait_ge(L["hid"], upto(*group))
                        if L["norm"] and (before := group_at(r, u, 4)):
                            pe.wait_ge(L["y"], upto(*before))
                        te.matmul(acc, ones_bf[:], L["b2"][:], start=True, stop=False)
                        for j in range(J):
                            last = te.matmul(acc[:, j, :], hid[s][:, j, :], L["w2"][:], start=False, stop=(j == J - 1))
                        last.then_inc(L["mm2"], 1)
                run(pe, step, 0, 2)

            gin(A)
            rows_stored(pe, A)
            gin(B)
            rows_stored(pe, B)

            def step_c(r, u):
                now, nxt, last = group_at(r, u, 0), group_at(r, u, -1), group_at(r, u, 1)
                if nxt:
                    s = nxt[1] % SLOTS
                    pe.wait_ge(C["gathered"][s], slot_uses(*nxt) * (16 * 2 * K))
                    pe.wait_ge(C["att"][s], slot_uses(*nxt) * (16 * K))
                    for rows, b in ((xsrc, 0), (xdst, 1), (xatt, 2)):
                        for k in range(K):
                            ins = te.transpose(by_k(banks[b])[:, k, :], rows[s][:, k, :], ident)
                    ins.then_inc(C["edgeT"], 1)
                if now:
                    pe.wait_ge(C["in"][u], 16 * (now[0] + 1))
                    for j in range(J):
                        ins = te.transpose(by_j(banks[5])[:, j, :], xin[u][:, j, :], ident)
                    ins.then_inc(C["xT"], 1)
                    pe.wait_ge(C["msg"], upto(*now))
                    pe.wait_ge(C["built"], upto(*now))
                    for k, (p0, p1) in enumerate(SPANS):
                        ins = te.matmul(by_j(banks[4])[:, :, p0:p1], msg[:, k, :], sel[u % 2][:, :, p0:p1], start=(k == 0), stop=(k == K - 1))
                    ins.then_inc(C["aggmm"], 1)
                if last:
                    acc = by_j(banks[7])
                    pe.wait_ge(C["hid"], upto(*last))
                    if before := group_at(r, u, 2):
                        pe.wait_ge(C["y"], upto(*before))
                    te.matmul(acc, ones_bf[:], brow_bf["b2"][:], start=True, stop=False)
                    for j in range(J):
                        ins = te.matmul(acc[:, j, :], hid[0][:, j, :], weights["W2"][:], start=False, stop=(j == J - 1))
                    ins.then_inc(C["w2"], 1)
                if nxt:
                    pe.wait_ge(C["srcT"], upto(*nxt))
                    pe.wait_ge(C["dstT"], upto(*nxt))
                    pe.wait_ge(C["attT"], upto(*nxt))
                    te.matmul(by_k(banks[1]), weights["Ws"][:], srcT[:], start=True, stop=False)
                    te.matmul(by_k(banks[1]), weights["Wd"][:], dstT[:], start=False, stop=False)
                    te.matmul(by_k(banks[1]), weights["Wa"][:], attT[:], start=False, stop=True)
                    te.matmul(by_k(banks[0]), weights["Wm"][:], srcT[:], start=True, stop=True).then_inc(C["gatemm"], 1)
                if now:
                    pe.wait_ge(C["xTs"], upto(*now))
                    te.matmul(by_j(banks[6]), weights["W1x"][:], hT[0][:], start=True, stop=False)
                    pe.wait_ge(C["aggT"], upto(*now))
                    te.matmul(by_j(banks[6]), weights["W1g"][:], aggT[:], start=False, stop=True).then_inc(C["w1"], 1)
                if nxt:
                    pe.wait_ge(C["msgT"], upto(*nxt))
                    for k in range(K):
                        ins = te.transpose(by_k(banks[3])[:, k, :], msgT[:, k, :], ident)
                    ins.then_inc(C["msgtr"], 1)
            run(pe, step_c, 1, 1)

        @block.scalar
        def _(act):
            a = nc.scalar
            act.wait_ge(v_setup, ready["all"])

            def normed(group, n, L, values, final, done, scaled):
                if group is None:
                    return
                r, u = group
                ln = ln_of(u)
                if u % 2 == 0:
                    act.wait_ge(L["chain"], scaled * LINKS)
                if final:
                    buffer_free(group, L)
                for j in range(J):
                    into = outt[u % SLOTS][:, j, :] if final else norm1[:, u % SLOTS, j, :]
                    c = n * PAIR + (u % 2) * J + j
                    last = a.activation(into, values[:, u % SLOTS, j, :], ACT.Identity, bias=ln["off"][:, c:c + 1], scale=ln["rstd"][:, c:c + 1])
                last.then_inc(done, 1)

            def buffer_free(group, L):
                r, u = group
                if not isinstance(r, int) or number(r, u) >= SLOTS:
                    act.wait_ge(L["stored"][u % SLOTS], (slot_uses(r, u) - 1) * 16)

            def gin(L):
                def step(r, u):
                    if group := group_at(r, u, 1):
                        s = group[1] % 2
                        act.wait_ge(L["mm1"], upto(*group))
                        a.activation(hid[s][:], by_j(banks[2 + s]), ACT.Relu, bias=L["b1"][:, 0:1]).then_inc(L["hid"], 1)
                    if L["norm"]:
                        if now := group_at(r, u, 0):
                            act.wait_ge(L["agg"], upto(*now))
                            a.copy(hT[u % 2][:], by_j(banks[u % 2])).then_inc(L["hT"], 1)
                        if old := group_at(r, u, 4):
                            normed(old, 0, L, y, True, L["out"], pairs_upto(old[0], old[1] + 1))
                    elif group := group_at(r, u, 2):
                        act.wait_ge(L["mm2"], upto(*group))
                        buffer_free(group, L)
                        a.activation(outt[group[1] % SLOTS][:], by_j(banks[4 + group[1] % 2]), ACT.Relu).then_inc(L["out"], 1)
                run(act, step, 0, 4 if L["norm"] else 2)

            gin(A)
            rows_stored(act, A)
            gin(B)
            rows_stored(act, B)

            def step_c(r, u):
                now, nxt, last = group_at(r, u, 0), group_at(r, u, -1), group_at(r, u, 1)
                if last:
                    act.wait_ge(C["w1"], upto(*last))
                    a.activation(sig[:], by_j(banks[6]), ACT.Sigmoid, bias=bias["b1"][:, 0:1]).then_inc(C["sig"], 1)
                if nxt:
                    act.wait_ge(C["edgeT"], upto(*nxt))
                    a.copy(srcT[:], by_k(banks[0])).then_inc(C["srcT"], 1)
                    a.copy(dstT[:], by_k(banks[1])).then_inc(C["dstT"], 1)
                    a.copy(attT[:], by_k(banks[2])).then_inc(C["attT"], 1)
                if now:
                    act.wait_ge(C["xT"], upto(*now))
                    a.copy(hT[0][:], by_j(banks[5])).then_inc(C["xTs"], 1)
                    act.wait_ge(C["aggmm"], upto(*now))
                    a.copy(aggT[:], by_j(banks[4])).then_inc(C["aggT"], 1)
                chains = (r * BODY + u - 2) // 2 if isinstance(r, int) else r * (BODY // 2) + u // 2 - 1
                normed(group_at(r, u, 8), 1, C, y2, True, C["out"], chains)
                normed(group_at(r, u, 4), 0, C, y, False, C["norm"], chains)
                if nxt:
                    act.wait_ge(C["gatemm"], upto(*nxt))
                    a.activation(gate[:], by_k(banks[1]), ACT.Sigmoid, bias=gate_bias[:, 0:1]).then_inc(C["gate"], 1)
            run(act, step_c, 1, 8)

        @block.gpsimd
        def _(pool):
            g = nc.gpsimd

            def by_index(dest, rows, index, done):
                g.indirect_dma_start(dest, None, rows, bass.IndirectOffsetOnAxis(ap=index, axis=0)).then_inc(done, 16)

            pool.wait_ge(v_setup, ready["row_i"])
            for b in range(BLOCKS):
                for half in range(2):
                    at = half * BLOCKS + b
                    for c, edge_list in enumerate((dst, src)):
                        by_index(lists_i[:, b, c, half * ROW:(half + 1) * ROW], edge_list.rearrange("(r c) -> r c", c=ROW), row_i[:, at:at + 1], s_rows)

            def gather(group, L):
                if group is None:
                    return
                pool.wait_ge(L["index"], upto(*group))
                pool.sem_inc(pool_turn, 1)
                s = group[1] % SLOTS
                for rows, idx in ((xsrc, src_idx), (xdst, dst_idx))[:2 if L is C else 1]:
                    for k in range(K):
                        by_index(rows[s][:, k, :], x1 if L is C else L["x"], idx[s][:, k:k + 1], L["gathered"][s])

            def layer(L):
                for g in range(SLOTS):
                    gather((0, g), L)
                run(pool, lambda r, u: gather(group_at(r, u, -SLOTS), L), 0, 0, exact=True)

            layer(A)
            rows_stored(pool, A)
            layer(B)
            rows_stored(pool, B)
            layer(C)

        @block.sync
        def _(sp):
            sp.dma_start(dst_rows[:], dst.rearrange("(r c) -> r c", c=ROW)).then_inc(s_dst, 16)
            sp.dma_start(consts[:], t["constants"]).then_inc(s_const, 16)
            for n in weights:
                sp.dma_start(weights[n][:], weight_src[n]).then_inc(s_wt, 16)
            for n in cols:
                sp.dma_start(bias[n][:], col_src[n].rearrange("(f o) -> f o", o=1)).then_inc(s_wt, 16)
            sp.wait_ge(v_setup, ready["brow"])
            for k, n in enumerate(rows3):
                for p in range(0, PARTS, 32):
                    sp.dma_start(brow[p:p + 1, k, :], row_src[n].rearrange("(o f) -> o f", o=1)).then_inc(s_wt, 16)
            for tile, vec in ((gamma, t["L1_gnn_gamma"]), (beta, t["L1_gnn_beta"])):
                sp.dma_start(tile[:], vec.partition_broadcast(P).rearrange("p (o f) -> p o f", o=1).to_broadcast([P, J, D])).then_inc(s_wt, 16)

            def layer(L, load, ahead, target, lag):
                def step(r, u):
                    load(group_at(r, u, -ahead), False)
                    if group := group_at(r, u, lag):
                        if number(*group) == GROUPS - 1 if isinstance(r, int) else False:
                            for s in range(SLOTS):
                                sp.wait_ge(L["stored"][s], 16 * len(range(s, GROUPS - 1, SLOTS)))
                        sp.wait_ge(L["out"], upto(*group))
                        sp.dma_start(node_rows(target, *group), outt[group[1] % SLOTS][:]).then_inc(L["stored"][group[1] % SLOTS], 16)
                for g in range(ahead):
                    load((0, g), True)
                run(sp, step, 0, lag, exact=True)
                rows_stored(sp, L)

            def load_a(group, fresh):
                if group is None:
                    return
                r, u = group
                if number(r, u) >= BODY if isinstance(r, int) else True:
                    sp.wait_ge(A["agg"], upto(r, u) - BODY)
                sp.dma_start(xin[u][:], node_rows(x, r, u)).then_inc(A["in"][u], 16)

            def load_b(group, fresh):
                if group is None:
                    return
                r, u = group
                if number(r, u) >= BODY if isinstance(r, int) else True:
                    sp.wait_ge(B["y"], upto(r, u) - BODY)
                sp.dma_start(xin[u][:], node_rows(h1, r, u)).then_inc(B["in"][u], 16)
                sp.dma_start(xres[u][:], node_rows(x, r, u)).then_inc(B["res"][u], 16)

            def load_c(group, fresh):
                if group is None:
                    return
                r, u = group
                if number(r, u) >= SLOTS if isinstance(r, int) else True:
                    sp.wait_ge(C["edgeT"], upto(r, u) - SLOTS)
                for k in range(K):
                    edge = sp.value_load(first_edge[0:1, bass.ds(number(r, u) * K + k, 1)], min_val=0, max_val=E - P)
                    sp.dma_start(xatt[u % SLOTS][:, k, :], attr[bass.ds(edge, P), :]).then_inc(C["att"][u % SLOTS], 16)
                if number(r, u) >= BODY if isinstance(r, int) else True:
                    sp.wait_ge(C["y2"], upto(r, u) - BODY)
                sp.dma_start(xin[u][:], node_rows(x1, r, u)).then_inc(C["in"][u], 16)

            layer(A, load_a, 6, h1, 3)
            layer(B, load_b, 6, x1, 5)
            sp.wait_ge(v_setup, ready["tables"])
            layer(C, load_c, SLOTS, out, 9)


_INS = ['x', 'src', 'dst', 'edge_attr_128',
        'L0_gnn_W1a', 'L0_gnn_b1a', 'L0_gnn_W2a', 'L0_gnn_b2a', 'L0_gnn_W1b', 'L0_gnn_b1b', 'L0_gnn_W2b', 'L0_gnn_b2b',
        'L1_gnn_Ws', 'L1_gnn_bs', 'L1_gnn_Wd', 'L1_gnn_bd', 'L1_gnn_Wa', 'L1_gnn_ba', 'L1_gnn_Wm', 'L1_gnn_bm',
        'L1_gnn_W1', 'L1_gnn_b1', 'L1_gnn_W2', 'L1_gnn_b2', 'L1_gnn_gamma', 'L1_gnn_beta']


def kernel(**inputs):
    import numpy as _np
    import concourse.bacc as _bacc
    from concourse import mybir as _mybir
    from concourse.bass_utils import run_bass_kernel_spmd as _run

    nc = _bacc.Bacc("TRN2", target_bir_lowering=False, num_devices=1)
    arrays, args = {}, {}
    given = {name: _np.ascontiguousarray(inputs[name]) for name in _INS}
    given["constants"] = constants()
    for name, a in given.items():
        arrays[f"in_{name}"] = a
        args[name] = nc.dram_tensor(f"in_{name}", a.shape, _mybir.dt.from_np(a.dtype), kind="ExternalInput").ap()
    out = nc.dram_tensor("out_0_dram", (N, D), F32, kind="ExternalOutput").ap()
    gnn_kernel(nc, args, out)
    r = _run(nc, [arrays], core_ids=[0])
    return r.results[0]["out_0_dram"]
```

```python
import numpy as np
import concourse.bass as bass
from concourse import mybir
from contextlib import ExitStack

F32 = mybir.dt.float32
BF16 = mybir.dt.bfloat16
I32 = mybir.dt.int32
ALU = mybir.AluOpType
ACT = mybir.ActivationFunctionType
AX = mybir.AxisListType

N, D, E = 50000, 128, 25000
EPS = 1e-5
NEWTON = 3
LINKS = 2 + 3 * NEWTON + 1
FIRST_LINKS = LINKS - 4
P = 128
J = 4
GROUP = P * J
GROUPS = -(-N // GROUP)
OVERLAP = GROUPS * GROUP - N
BODY = 8
ROUNDS = GROUPS // BODY
SLOTS = 4
SPANS = [(0, 43), (43, 86), (86, P)]
K = len(SPANS)
WIDTH = J * 43
BLOCKS = -(-GROUPS * K // P)
ROW = 200
ROWS = E // ROW
SHIFTS = [1 << b for b in range(ROW.bit_length() - 1, -1, -1)]
assert GROUPS % 2 == 0 and ROW * ROWS == E and ROWS <= P
assert ROW + P <= 2 * ROW and sum(SHIFTS) + P <= 2 * ROW
AFTER_LAST = 1 << 30


def group_base(g):
    return max(g * GROUP - OVERLAP, 0)


def constants():
    starts = np.full(BLOCKS * P, N, np.float32)
    for g in range(GROUPS):
        for k, (p0, _) in enumerate(SPANS):
            starts[K * g + k] = group_base(g) + J * p0
    rows = np.broadcast_to(starts, (P, BLOCKS * P))
    ends = np.full(BLOCKS * P, N, np.float32)
    for g in range(GROUPS):
        for k, (_, p1) in enumerate(SPANS):
            ends[K * g + k] = group_base(g) + J * p1
    by_part = starts.reshape(BLOCKS, P).T
    ends_by_part = ends.reshape(BLOCKS, P).T
    local = (J * np.arange(WIDTH // J)[None, :] + np.arange(J)[:, None]).reshape(-1)
    local = np.broadcast_to(local, (P, WIDTH))
    return np.ascontiguousarray(np.concatenate([rows, by_part, ends_by_part, local, np.eye(P)], 1).astype(np.float32))


def pair_constants():
    follows = np.triu(np.ones((ROWS, ROWS)), 1)
    spare = N + np.arange(ROWS)[:, None]
    return np.ascontiguousarray(np.concatenate([follows, spare], 1).astype(np.float32))


CONST_COLS = BLOCKS * P + 2 * BLOCKS + WIDTH + P


def gnn_kernel(nc, t, out):
    ctx = ExitStack()
    with ctx:
        def sb(name, shape, dt=F32):
            return ctx.enter_context(nc.sbuf_tensor(name, shape, dt))

        def sem(name):
            return ctx.enter_context(nc.semaphore(name))

        def sems(stage, names):
            return {n: sem(f"{stage}_{n}") for n in names.split()}

        def slot_sems(name, slots=SLOTS):
            return [sem(f"{name}{u}") for u in range(slots)]

        x, src, dst, attr = t["x"], t["src"], t["dst"], t["edge_attr_128"]
        h1 = nc.dram_tensor("h1", (N, D), F32, kind="Internal").ap()
        x1 = nc.dram_tensor("x1", (N, D), F32, kind="Internal").ap()
        sums = nc.dram_tensor("sums", (N + P, D), F32, kind="Internal").ap()

        consts = sb("consts", [P, CONST_COLS])
        o = 0
        starts_row = consts[:, o:o + BLOCKS * P]
        o += BLOCKS * P
        starts_part = consts[:, o:o + BLOCKS]
        o += BLOCKS
        ends_part = consts[:, o:o + BLOCKS]
        o += BLOCKS
        local_node = consts[:, o:o + WIDTH].rearrange("p (j q) -> p j q", j=J)
        o += WIDTH
        ident = consts[:, o:o + P]

        dst_rows = sb("dst_rows", [ROWS, ROW], I32)
        src_rows = sb("src_rows", [ROWS, ROW], I32)
        next_row = sb("next_row", [ROWS, 8], I32)
        dst_f = sb("dst_f", [ROWS, ROW + 1])
        falls = sb("falls", [ROWS, ROW])
        falls_in_row = sb("falls_in_row", [P, 1])
        over = sb("over", [P, BLOCKS])
        early = sb("early", [P, BLOCKS])
        over_all = sb("over_all", [P, 1])
        any_edges = sb("any_edges", [1, 1], I32)

        row_last = sb("row_last", [ROWS, 1])
        row_before = sb("row_before", [ROWS, BLOCKS * P])
        ones = sb("ones", [P, 1])
        row_f = sb("row_f", [P, 2 * BLOCKS])
        row_i = sb("row_i", [P, 2 * BLOCKS], I32)
        lists_i = sb("lists_i", [P, BLOCKS, 2, 2 * ROW], I32)
        lists = sb("lists", [P, BLOCKS, 2, P])
        smaller = sb("smaller", [P, BLOCKS, ROW])
        shift = sb("shift", [P, BLOCKS])
        room = sb("room", [P, BLOCKS])
        shift_i = sb("shift_i", [P, BLOCKS], I32)
        bits = sb("bits", [P, len(SHIFTS), BLOCKS], I32)
        first = sb("first", [P, BLOCKS])
        first_edge = sb("first_edge", [1, BLOCKS * P], I32)
        dst_local = sb("dst_local", [P, BLOCKS * P])
        edge_nodes = sb("edge_nodes", [P, 2, BLOCKS * P], I32)

        weights = {n: sb(n, [D, D]) for n in ("W1a", "W2a", "W1b", "W2b", "Ws", "Wd", "Wa", "Wm", "W1x", "W1g", "W2")}
        weight_src = {
            "W1a": t["L0_gnn_W1a"], "W2a": t["L0_gnn_W2a"], "W1b": t["L0_gnn_W1b"], "W2b": t["L0_gnn_W2b"],
            "Ws": t["L1_gnn_Ws"], "Wd": t["L1_gnn_Wd"], "Wa": t["L1_gnn_Wa"], "Wm": t["L1_gnn_Wm"],
            "W1x": t["L1_gnn_W1"][0:D, :], "W1g": t["L1_gnn_W1"][D:2 * D, :], "W2": t["L1_gnn_W2"]}
        cols = ("b1a", "b1b", "bs", "bd", "ba", "bm", "b1")
        col_src = {"b1a": t["L0_gnn_b1a"], "b1b": t["L0_gnn_b1b"], "bs": t["L1_gnn_bs"], "bd": t["L1_gnn_bd"],
                   "ba": t["L1_gnn_ba"], "bm": t["L1_gnn_bm"], "b1": t["L1_gnn_b1"]}
        bias = {n: sb(f"col_{n}", [D, 1]) for n in cols}
        gate_bias = sb("gate_bias", [D, 1])
        rows3 = ("b2b", "b2")
        row_src = {"b2b": t["L0_gnn_b2b"], "b2": t["L1_gnn_b2"]}
        PARTS = 65
        brow = sb("brow", [PARTS, len(rows3), D])
        brest = sb("brest", [PARTS, len(rows3), D])
        bpart = sb("bpart", [PARTS, len(rows3), D], BF16)
        brow_all = sb("brow_all", [PARTS, len(rows3), D], BF16)
        brow_bf = {n: brow_all[:, k:k + 1, :].to_broadcast([PARTS, J, D]) for k, n in enumerate(rows3)}
        ones_bf = sb("ones_bf", [PARTS, P], BF16)
        gamma = sb("gamma", [P, J, D])
        beta = sb("beta", [P, J, D])
        b2a = sb("b2a", [P, 1, D])

        xin = [sb(f"xin{u}", [P, J, D]) for u in range(BODY)]
        xres = [sb(f"xres{u}", [P, J, D]) for u in range(BODY)]
        xsrc = [sb(f"xsrc{u}", [P, K, D]) for u in range(SLOTS)]
        xdst = [sb(f"xdst{u}", [P, K, D]) for u in range(SLOTS)]
        xatt = [sb(f"xatt{u}", [P, K, D]) for u in range(SLOTS)]
        outt = [sb(f"outt{u}", [P, J, D]) for u in range(SLOTS)]
        index = [sb(f"index{u}", [P, 2, K], I32) for u in range(SLOTS)]
        src_idx, dst_idx = ([i[:, c, :] for i in index] for c in range(2))
        sel = [sb(f"sel{s}", [P, J, P]) for s in range(2)]
        hT = [sb(f"hT{s}", [P, J, P]) for s in range(2)]
        hid = [sb(f"hid{s}", [P, J, P]) for s in range(2)]
        ysum = sb("ysum", [P, BODY, J, D])
        y, y2 = ysum[:, 0:SLOTS], ysum[:, SLOTS:]
        norm1 = sb("norm1", [P, SLOTS, J, D])
        srcT = sb("srcT", [P, K, P])
        dstT = sb("dstT", [P, K, P])
        attT = sb("attT", [P, K, P])
        gate = sb("gate", [P, K, P])
        msgT = sb("msgT", [P, K, P])
        msg = sb("msg", [P, K, P])
        aggT = sb("aggT", [P, J, P])
        sig = sb("sig", [P, J, P])
        pairs = sb("pairs", [ROWS, ROWS + 1])
        follows, spare = pairs[:, 0:ROWS], pairs[:, ROWS:]
        again = sb("again", [ROWS, ROWS])
        repeats = sb("repeats", [ROWS, 1])
        to_spare = sb("to_spare", [ROWS, 1])
        keep_i = sb("keep_i", [ROWS, 1], I32)
        goes_to = sb("goes_to", [ROWS, 1])
        wide = sb("wide", [ROWS, ROWS])
        same = sb("same", [ROWS, ROWS])
        PAIR = 2 * J
        LN = [{"stats": sb(f"stats{p}", [P, 2, PAIR, 6]), "rest": sb(f"rest{p}", [P, 2 * PAIR]), "half": sb(f"half{p}", [P, 2 * PAIR], I32),
               **{part: sb(f"{part}{p}", [P, 2 * PAIR]) for part in ("sum", "dif", "var", "rstd", "off")}} for p in range(2)]

        banks = [ctx.enter_context(nc.psum_tensor(f"bank{b}", [P, GROUP], F32)) for b in range(8)]

        def by_j(b):
            return b[:, :].rearrange("p (j q) -> p j q", j=J)

        def by_k(b):
            return b[:, 0:K * P].rearrange("p (k q) -> p k q", k=K)

        s_const, s_dst, s_next, s_wt, s_first = (sem(n) for n in ("s_const", "s_dst", "s_next", "s_wt", "s_first"))
        s_rows = [sem("s_dst_rows"), sem("s_src_rows")]
        v_setup, pe_setup, pool_setup, pool_turn = sem("v_setup"), sem("pe_setup"), sem("pool_setup"), sem("pool_turn")

        def layer_sems(name, names):
            return {"name": name, **sems(name, names), "in": slot_sems(f"{name}_in", BODY),
                    "gathered": slot_sems(f"{name}_gathered"), "stored": slot_sems(f"{name}_stored")}

        GIN = "index built agg hT mm1 hid mm2 out"
        A = {**layer_sems("a", GIN + " y"), "x": x, "w1": weights["W1a"], "b1": bias["b1a"], "w2": weights["W2a"], "norm": False, "any": False, "no": 0}
        B = {**layer_sems("b", GIN + " y stats dif var chain"), "res": slot_sems("b_res", BODY),
             "x": h1, "w1": weights["W1b"], "b1": bias["b1b"], "w2": weights["W2b"], "b2": brow_bf["b2b"], "norm": True, "any": False, "no": 1}
        C = {**layer_sems("c", "index built edgeT srcT dstT attT logits gatemm gate msgT msgmm msg xT xTs sumT aggT w1 sig hid w2 y "
                          "stats dif var norm ga gb y2 stats2 chain out"),
             "att": slot_sems("c_att"), "res": slot_sems("c_res", BODY), "x": x1, "any": False, "no": 2}
        A_any, B_any, C_any = ({**L, "any": True} for L in (A, B, C))
        G = sems("any", "filled zero turn index wide across same again repeats keep rows att edgeT rowsT gatemm gate msgT msgtr msg summed old new scattered")
        s_any = sem("s_any")
        block = ctx.enter_context(nc.Block())

        def group_at(r, u, lag):
            n = u - lag
            group = (r + n // BODY, n % BODY)
            if isinstance(r, int) and not 0 <= number(*group) < GROUPS:
                return None
            return group

        def number(r, u):
            return r * BODY + u

        def upto(r, u):
            return r * BODY + u + 1

        def slot_uses(r, u):
            return r * (BODY // SLOTS) + u // SLOTS + 1

        def pairs_upto(r, u):
            return r * (BODY // 2) + (u + 1) // 2

        def ln_of(u):
            return LN[u // 2 % 2]

        def run(eng, step, lead, lag, exact=False, apart=0):
            first = max(1, -(-(lag + apart) // BODY))
            for g in range(-lead, first * BODY):
                step(g // BODY, g % BODY)
            last = ROUNDS - (1 if exact else 0)
            with eng.Fori(first, last) as r:
                for u in range(BODY):
                    step(r, u)
            for g in range(last * BODY, GROUPS + lag):
                step(g // BODY, g % BODY)

        def node_rows(dram, r, u):
            base = group_base(number(r, u)) if isinstance(r, int) else r * (BODY * GROUP) + (u * GROUP - OVERLAP)
            return dram[bass.ds(base, GROUP), :].rearrange("(p j) f -> p j f", j=J)

        def rows_stored(eng, L):
            for s in range(SLOTS):
                eng.wait_ge(L["stored"][s], 16 * len(range(s, GROUPS, SLOTS)))

        def tile_no(L, t):
            return t + (L["no"] * ROW + 1)

        def turn(L, t):
            return t + (L["no"] * (ROW + 1) + 1)

        BIAS_STEPS = 1 + 2 + 3 * 2 + 2

        def run_layers(eng, layers):
            eng.wait_ge(pool_setup, BIAS_STEPS)
            eng.wait_ge(v_setup, ready["all"])
            irregular = eng.value_load(any_edges[0:1, 0:1], min_val=0, max_val=1)
            with eng.If(irregular > 0):
                layers(A_any, B_any, C_any)
            with eng.Else():
                layers(A, B, C)


        ready = {}

        @block.vector
        def _(dve):
            v = nc.vector
            count = [0]

            def step(ins):
                count[0] += 1
                ins.then_inc(v_setup, 1)
                dve.wait_ge(v_setup, count[0])

            step(v.memset(next_row[:], AFTER_LAST))
            step(v.memset(brow[:], 0.0))
            step(v.memset(brow_all[:], 0.0))
            ready["brow"] = count[0]
            step(v.memset(ones[:], 1.0))
            dve.wait_ge(s_dst, 16)
            step(v.tensor_copy(row_last[:], dst_rows[:, ROW - 1:ROW]))
            dve.wait_ge(s_const, 16)
            step(v.tensor_scalar(row_before[:], starts_row[0:ROWS, :], row_last[:, 0:1], None, ALU.is_gt))
            ready["row_before"] = count[0]
            dve.wait_ge(pe_setup, 1)
            step(v.tensor_scalar(row_f[:, 0:BLOCKS], banks[0][:, 0:BLOCKS], float(ROWS - 1), None, ALU.min))
            step(v.tensor_scalar(row_f[:, BLOCKS:], banks[0][:, 0:BLOCKS], 1.0, float(ROWS - 1), ALU.add, ALU.min))
            step(v.tensor_copy(row_i[:], row_f[:]))
            ready["row_i"] = count[0]
            dve.wait_ge(s_next, 16)
            step(v.tensor_copy(dst_f[:, 0:ROW], dst_rows[:]))
            step(v.tensor_copy(dst_f[:, ROW:], next_row[:, 0:1]))
            step(v.tensor_tensor(falls[:], dst_f[:, 0:ROW], dst_f[:, 1:], ALU.is_gt))
            step(v.memset(falls_in_row[:], 0.0))
            step(v.tensor_reduce(falls_in_row[0:ROWS, :], falls[:], AX.X, ALU.add))
            for p in range(2):
                step(v.memset(LN[p]["stats"][:], 1.0))
            dve.wait_ge(s_first, 16 * BLOCKS)
            for b in range(BLOCKS):
                step(v.tensor_scalar(smaller[:, b, :], lists_i[:, b, 0, 0:ROW], starts_part[:, b:b + 1], None, ALU.is_lt))
            step(v.tensor_reduce(shift[:], smaller[:], AX.X, ALU.add))
            step(v.tensor_scalar(room[:], row_f[:, 0:BLOCKS], float(ROWS - 1), -float(P), ALU.is_ge, ALU.mult))
            step(v.tensor_scalar(room[:], room[:], float(ROW), None, ALU.add))
            step(v.tensor_tensor(shift[:], shift[:], room[:], ALU.min))
            step(v.scalar_tensor_tensor(first[:], row_f[:, 0:BLOCKS], float(ROW), shift[:], ALU.mult, ALU.add))
            step(v.tensor_copy(shift_i[:], shift[:]))
            for k, n in enumerate(SHIFTS):
                step(v.tensor_single_scalar(bits[:, k, :], shift_i[:], n, ALU.bitwise_and))
            for c in range(2):
                dve.wait_ge(s_rows[c], 16 * (c + 1) * BLOCKS)
                for k, n in enumerate(SHIFTS):
                    width = P + n - 1
                    mask = bits[:, k, :].rearrange("p (b o) -> p b o", o=1).to_broadcast([P, BLOCKS, width])
                    step(v.copy_predicated(lists_i[:, :, c, 0:width], mask, lists_i[:, :, c, n:n + width]))
            step(v.tensor_copy(lists[:], lists_i[:, :, :, 0:P]))
            ready["lists"] = count[0]
            step(v.tensor_tensor(over[:], lists[:, :, 0, P - 1], ends_part, ALU.is_lt))
            step(v.tensor_scalar(early[:], first[:], float(E - P), None, ALU.is_lt))
            step(v.tensor_tensor(over[:], over[:], early[:], ALU.mult))
            step(v.tensor_reduce(over_all[:], over[:], AX.X, ALU.add))
            step(v.tensor_tensor(over_all[:], over_all[:], falls_in_row[:], ALU.add))
            ready["over"] = count[0]
            dve.wait_ge(pe_setup, 2)
            flat = banks[1][:, 0:BLOCKS * P]
            step(v.tensor_copy(edge_nodes[:, 1, :], flat))
            step(v.tensor_tensor(dst_local[:], flat, starts_row, ALU.subtract))
            step(v.tensor_copy(edge_nodes[:, 0, :], banks[2][:, 0:BLOCKS * P]))
            step(v.tensor_copy(first_edge[:], banks[3][0:1, 0:BLOCKS * P]))
            ready["tables"] = count[0]
            dve.wait_ge(pe_setup, 3)
            step(v.tensor_scalar(any_edges[:], banks[4][0:1, 0:1], 0.5, None, ALU.is_gt))
            ready["all"] = count[0]

            def stage_index(group, L):
                if group is None or L["any"]:
                    return
                r, u = group
                v.tensor_copy(index[u % SLOTS][:], edge_nodes[:, :, bass.ds(number(r, u) * K, K)]).then_inc(L["index"], 1)

            def build(group, L, only=None):
                if group is None or L["any"]:
                    return
                r, u = group
                for k, (p0, p1) in enumerate(SPANS):
                    if only is not None and k != only:
                        continue
                    goes_to = dst_local[:, bass.ds(number(r, u) * K + k, 1)]
                    last = v.tensor_scalar(sel[u % 2][:, :, p0:p1], local_node[:, :, 0:p1 - p0], goes_to, None, ALU.is_equal)
                if only in (None, K - 1):
                    last.then_inc(L["built"], 1)

            def row_stats(values, slot, u, n, done, between=lambda: None):
                for j in range(J):
                    if j > 0:
                        between()
                    last = v.bn_stats(ln_of(u)["stats"][:, n, (u % 2) * J + j, :], values[:, slot, j, :])
                last.then_inc(done, 1)

            def moments(pair, no, L, cols, waits, parts=(0, 1, 2)):
                if pair is None:
                    return
                ln = ln_of(pair[1])
                st = ln["stats"][:].rearrange("p n c s -> p (n c) s")[:, 0:cols]
                total, dif, var = (ln[part][:, 0:cols] for part in ("sum", "dif", "var"))
                if 0 in parts:
                    for name, value in waits:
                        dve.wait_ge(L[name], value)
                    v.tensor_tensor(total, st[:, :, 1], st[:, :, 4], ALU.add)
                    v.tensor_tensor(dif, st[:, :, 1], st[:, :, 4], ALU.subtract)
                    v.scalar_tensor_tensor(var, st[:, :, 2], D * EPS, st[:, :, 5], ALU.add, ALU.add).then_inc(L["dif"], 1)
                if 1 in parts:
                    dve.wait_ge(L["dif"], no * 2 - 1)
                    v.scalar_tensor_tensor(dif, dif, 0.25, dif, ALU.mult, ALU.mult).then_inc(L["dif"], 1)
                if 2 in parts:
                    dve.wait_ge(L["dif"], no * 2)
                    v.scalar_tensor_tensor(var, var, 1.0 / D, dif, ALU.mult, ALU.add).then_inc(L["var"], 1)

            class Scales:

                def __init__(self, group, chain_no, L, cols, var_done, at=0):
                    self.group, self.no, self.L, self.cols, self.at, self.var_done = group, chain_no, L, cols, at, var_done

                def go(self, links=1):
                    if self.group is None:
                        return
                    ln = ln_of(self.group[1])
                    c = slice(0, self.cols)
                    for _ in range(links):
                        n, self.at = self.at, self.at + 1
                        if n == 0:
                            for name, value in self.var_done:
                                dve.wait_ge(self.L[name], value)
                        else:
                            dve.wait_ge(self.L["chain"], self.no * LINKS - (LINKS - n))
                        if n == 0:
                            ins = v.tensor_single_scalar(ln["half"][:, c], ln["var"][:, c].bitcast(I32), 1, ALU.logical_shift_right)
                        elif n == 1:
                            ins = v.tensor_scalar(ln["rstd"][:, c].bitcast(I32), ln["half"][:, c], -1.0, float(0x5F3759DF), ALU.mult, ALU.add)
                        elif n == LINKS - 1:
                            ins = v.scalar_tensor_tensor(ln["off"][:, c], ln["sum"][:, c], -0.5, ln["rstd"][:, c], ALU.mult, ALU.mult)
                        elif n % 3 == 2:
                            ins = v.tensor_tensor(ln["rest"][:, c], ln["rstd"][:, c], ln["rstd"][:, c], ALU.mult)
                        elif n % 3 == 0:
                            ins = v.scalar_tensor_tensor(ln["rest"][:, c], ln["rest"][:, c], -0.5, ln["var"][:, c], ALU.mult, ALU.mult)
                        else:
                            ins = v.scalar_tensor_tensor(ln["rstd"][:, c], ln["rest"][:, c], 1.5, ln["rstd"][:, c], ALU.add, ALU.mult)
                        ins.then_inc(self.L["chain"], 1)

                def end(self):
                    self.go(LINKS - self.at)

            def layer_ended(L, begin_next):
                if not L["any"]:
                    dve.wait_ge(L["index"], GROUPS + 2)
                    dve.wait_ge(L["built"], GROUPS)
                    begin_next()
                rows_stored(dve, L)

            def begin_gin(L):
                for g in range(SLOTS):
                    stage_index((0, g), L)
                for g in range(2):
                    build((0, g), L)

            def begin_c(C):
                for g in range(SLOTS - 1):
                    stage_index((0, g), C)

            def edge_sums(L):
                if L["no"] == 2:
                    v.memset(norm1[0:ROWS, 0, 0, :], 0.0).then_inc(G["zero"], 1)
                with dve.Fori(0, ROW) as t:
                    n = tile_no(L, t)
                    dve.wait_ge(G["turn"], turn(L, t))
                    v.tensor_copy(src_idx[0][0:ROWS, 0:1], src_rows[:, bass.ds(t, 1)])
                    v.tensor_copy(dst_idx[0][0:ROWS, 0:1], dst_rows[:, bass.ds(t, 1)])
                    v.tensor_copy(goes_to[:], dst_rows[:, bass.ds(t, 1)]).then_inc(G["index"], 1)
                    dve.wait_ge(G["index"], n)
                    v.tensor_scalar(wide[:], ident[0:ROWS, 0:ROWS], 0.0, goes_to[:, 0:1], ALU.mult, ALU.add).then_inc(G["wide"], 1)
                    dve.wait_ge(G["across"], n)
                    v.tensor_scalar(same[:], banks[7][0:ROWS, 0:ROWS], goes_to[:, 0:1], None, ALU.is_equal).then_inc(G["same"], 1)
                    dve.wait_ge(G["same"], n)
                    v.tensor_tensor(again[:], same[:], follows, ALU.mult).then_inc(G["again"], 1)
                    dve.wait_ge(G["again"], n)
                    v.tensor_reduce(repeats[:], again[:], AX.X, ALU.max)
                    v.tensor_tensor(to_spare[:], spare, goes_to[:], ALU.subtract).then_inc(G["repeats"], 1)
                    dve.wait_ge(G["repeats"], n)
                    v.scalar_tensor_tensor(keep_i[:], to_spare[:], repeats[:, 0:1], goes_to[:], ALU.mult, ALU.add).then_inc(G["keep"], 1)
                    if L["no"] == 2:
                        dve.wait_ge(G["gate"], t + 1)
                        v.scalar_tensor_tensor(msgT[:, 0, 0:ROWS], banks[0][:, 0:ROWS], bias["bm"][:, 0:1], gate[:, 0, 0:ROWS], ALU.add, ALU.mult).then_inc(G["msgT"], 1)
                        dve.wait_ge(G["msgtr"], t + 1)
                        v.tensor_copy(msg[0:ROWS, 0, :], banks[3][0:ROWS, 0:D]).then_inc(G["msg"], 1)
                    dve.wait_ge(G["summed"], n)
                    dve.wait_ge(G["old"], n * 16)
                    v.tensor_tensor(y[0:ROWS, 0, 0, :], banks[4][0:ROWS, 0:D], xres[0][0:ROWS, 0, :], ALU.add).then_inc(G["new"], 1)
                dve.wait_ge(G["turn"], turn(L, ROW))

            def gin(L):
                def step(r, u):
                    if not L["norm"]:
                        if now := group_at(r, u, 0):
                            dve.wait_ge(L["agg"], upto(*now))
                            v.tensor_copy(hT[u % 2][:], by_j(banks[u % 2])).then_inc(L["hT"], 1)
                        stage_index(group_at(r, u, -SLOTS), L)
                        build(group_at(r, u, -2), L)
                        if last := group_at(r, u, 3):
                            lr, lu = last
                            dve.wait_ge(L["mm2"], upto(lr, lu))
                            v.tensor_tensor(xres[lu][:], by_j(banks[4 + lu % SLOTS]), b2a[:].to_broadcast([P, J, D]), ALU.add).then_inc(L["y"], 1)
                        return
                    odd = u % 2 == 1
                    ended = group_at(r, u, 4 if odd else 5)
                    normed = group_at(r, u, 8) if odd else None
                    waits = [("var", pairs_upto(*ended))] if ended else []
                    if normed:
                        waits.append(("out", upto(*normed)))
                    scales = Scales(ended, pairs_upto(*ended) if ended else 0, L, PAIR, waits, at=0 if odd else FIRST_LINKS)
                    ended_now = ended if odd else None
                    if last := group_at(r, u, 3):
                        lr, lu = last
                        dve.wait_ge(L["res"][lu], 16 * (lr + 1))
                        dve.wait_ge(L["mm2"], upto(lr, lu))
                        v.scalar_tensor_tensor(ysum[:, lu], by_j(banks[4 + lu % SLOTS]), 0.0, xres[lu][:], ALU.max, ALU.add).then_inc(L["y"], 1)
                    pairs = pairs_upto(*ended_now) if ended_now else 0
                    moments(ended_now, pairs, L, PAIR, [], parts=(1,))
                    if not odd:
                        scales.go()
                    if now := group_at(r, u, 0):
                        dve.wait_ge(L["agg"], upto(*now))
                    stage_index(group_at(r, u, -SLOTS), L)
                    moments(ended_now, pairs, L, PAIR, [], parts=(2,))
                    nxt = group_at(r, u, -2)
                    for k in range(K):
                        if not odd:
                            scales.go()
                        build(nxt, L, k)
                        if odd:
                            scales.go()
                    if last:
                        dve.wait_ge(L["y"], upto(lr, lu))
                        row_stats(ysum, lu, lu, 0, L["stats"], scales.go if odd else lambda: None)
                    if odd:
                        scales.go(FIRST_LINKS - scales.at)
                    else:
                        moments(last, 0, L, PAIR, [("stats", upto(*last))] if last else [], parts=(0,))
                run(dve, step, 0, 5 if L["norm"] else 3)

            def step_c(C, r, u):
                now, nxt, last, old = group_at(r, u, 0), group_at(r, u, -1), group_at(r, u, 1), group_at(r, u, 5)
                odd = u % 2 == 1
                either = (group_at(r, u, 2) or group_at(r, u, 6)) if odd else None
                no = (r * BODY + u) // 2 if isinstance(r, int) else r * (BODY // 2) + u // 2
                scales = Scales(either, no, C, 2 * PAIR, [("var", no)])

                def residual_2():
                    if old:
                        dve.wait_ge(C["gb"], upto(*old))
                        v.tensor_tensor(y2[:, ou], norm1[:, ou], xin[old[1]][:], ALU.add).then_inc(C["y2"], 1)

                def message():
                    if nxt and not C["any"]:
                        dve.wait_ge(C["gate"], upto(*nxt))
                        dve.wait_ge(C["gatemm"], upto(*nxt))
                        v.scalar_tensor_tensor(msgT[:], by_k(banks[1]), bias["bm"][:, 0:1], gate[:], ALU.add, ALU.mult).then_inc(C["msgT"], 1)

                if last:
                    dve.wait_ge(C["sig"], upto(*last))
                    v.scalar_tensor_tensor(hid[0][:], by_j(banks[6]), bias["b1"][:, 0:1], sig[:], ALU.add, ALU.mult).then_inc(C["hid"], 1)
                elif now and not C["any"]:
                    dve.wait_ge(C["gathered"][0], 16 * 2 * K)
                moments(either, no, C, 2 * PAIR, [], parts=(1,))
                stage_index(group_at(r, u, -SLOTS), C)
                moments(either, no, C, 2 * PAIR, [], parts=(2,))
                for k in range(K):
                    build(nxt, C, k)
                    scales.go()
                if old:
                    ou = old[1] % SLOTS
                    dve.wait_ge(C["norm"], upto(*old))
                    v.tensor_tensor(norm1[:, ou], norm1[:, ou], gamma[:], ALU.mult).then_inc(C["ga"], 1)
                scales.go()
                if last:
                    lu = last[1]
                    dve.wait_ge(C["w2"], upto(*last))
                    v.tensor_tensor(y[:, lu % SLOTS], by_j(banks[7]), xin[lu][:], ALU.add).then_inc(C["y"], 1)
                scales.go()
                if old:
                    dve.wait_ge(C["ga"], upto(*old))
                    v.tensor_tensor(norm1[:, ou], norm1[:, ou], beta[:], ALU.add).then_inc(C["gb"], 1)
                scales.go()
                if last:
                    dve.wait_ge(C["y"], upto(*last))
                    row_stats(y, lu % SLOTS, lu, 0, C["stats"], scales.go)
                scales.go()
                if not odd:
                    residual_2()
                message()
                scales.go()
                if odd:
                    residual_2()
                scales.end()
                if old:
                    dve.wait_ge(C["y2"], upto(*old))
                    row_stats(y2, ou, old[1], 1, C["stats2"])
                if not odd:
                    waits = [(name, upto(*group)) for name, group in (("stats", last), ("stats2", old)) if group]
                    moments(last or old, 0, C, 2 * PAIR, waits, parts=(0,))

            def layers(A, B, C):
                if A["any"]:
                    dve.wait_ge(s_any, 16 * 2)
                    edge_sums(A)
                begin_gin(A)
                gin(A)
                layer_ended(A, lambda: begin_gin(B))
                if B["any"]:
                    edge_sums(B)
                gin(B)
                layer_ended(B, lambda: begin_c(C))
                if C["any"]:
                    edge_sums(C)
                run(dve, lambda r, u: step_c(C, r, u), 1, 6)

            run_layers(dve, layers)

        @block.tensor
        def _(pe):
            te = nc.tensor
            pe.wait_ge(v_setup, ready["row_before"])
            for b in range(BLOCKS):
                last = te.matmul(banks[0][:, b:b + 1], row_before[:, b * P:(b + 1) * P], ones[0:ROWS, :], start=True, stop=True)
            last.then_inc(pe_setup, 1)
            pe.wait_ge(v_setup, ready["lists"])
            for b in range(BLOCKS):
                at = slice(b * P, (b + 1) * P)
                te.transpose(banks[1][:, at], lists[:, b, 0, 0:P], ident)
                te.transpose(banks[2][:, at], lists[:, b, 1, 0:P], ident)
                last = te.transpose(banks[3][0:1, at], first[:, b:b + 1], ident)
            last.then_inc(pe_setup, 1)
            pe.wait_ge(v_setup, ready["over"])
            te.matmul(banks[4][0:1, 0:1], over_all[:], ones[:], start=True, stop=True).then_inc(pe_setup, 1)

            def edge_sums(L):
                rows_of = 32 if L["no"] == 2 else 16
                with pe.Fori(0, ROW) as t:
                    n = tile_no(L, t)
                    pe.wait_ge(G["wide"], n)
                    te.transpose(banks[7][0:ROWS, 0:ROWS], wide[:], ident[0:ROWS, 0:ROWS]).then_inc(G["across"], 1)
                    pe.wait_ge(G["rows"], (t + 1) * rows_of + L["no"] * (16 * ROW))
                    if L["no"] == 2:
                        pe.wait_ge(G["att"], (t + 1) * 16)
                        for rows, b in ((xsrc, 0), (xdst, 1), (xatt, 2)):
                            ins = te.transpose(banks[b][:, 0:ROWS], rows[0][0:ROWS, 0, :], ident[0:ROWS, 0:ROWS])
                        ins.then_inc(G["edgeT"], 1)
                        pe.wait_ge(G["rowsT"], t + 1)
                        te.matmul(banks[1][:, 0:ROWS], weights["Ws"][:], srcT[:, 0, 0:ROWS], start=True, stop=False)
                        te.matmul(banks[1][:, 0:ROWS], weights["Wd"][:], dstT[:, 0, 0:ROWS], start=False, stop=False)
                        te.matmul(banks[1][:, 0:ROWS], weights["Wa"][:], attT[:, 0, 0:ROWS], start=False, stop=True)
                        te.matmul(banks[0][:, 0:ROWS], weights["Wm"][:], srcT[:, 0, 0:ROWS], start=True, stop=True).then_inc(G["gatemm"], 1)
                        pe.wait_ge(G["msgT"], t + 1)
                        te.transpose(banks[3][0:ROWS, 0:D], msgT[:, 0, 0:ROWS], ident).then_inc(G["msgtr"], 1)
                        pe.wait_ge(G["msg"], t + 1)
                    pe.wait_ge(G["same"], n)
                    values = msg if L["no"] == 2 else xsrc[0]
                    te.matmul(banks[4][0:ROWS, 0:D], same[:], values[0:ROWS, 0, :], start=True, stop=True).then_inc(G["summed"], 1)
                pe.wait_ge(G["turn"], turn(L, ROW))

            def gin(L):
                def step(r, u):
                    if now := group_at(r, u, 0):
                        acc = by_j(banks[u % 2])
                        if not L["any"]:
                            pe.wait_ge(L["built"], upto(*now))
                            pe.wait_ge(L["gathered"][u % SLOTS], slot_uses(*now) * (16 * K))
                            for k, (p0, p1) in enumerate(SPANS):
                                te.matmul(acc[:, :, p0:p1], xsrc[u % SLOTS][:, k, :], sel[u % 2][:, :, p0:p1], start=(k == 0), stop=False)
                        pe.wait_ge(L["in"][u], 16 * (now[0] + 1))
                        for j in range(J):
                            last = te.matmul(acc[:, j, :], xin[u][:, j, :], ident, start=L["any"], stop=(L["any"] or j == J - 1), is_transpose=True)
                        last.then_inc(L["agg"], 1)
                    if group := group_at(r, u, 1):
                        s = group[1] % 2
                        pe.wait_ge(L["hT"], upto(*group))
                        te.matmul(by_j(banks[2 + s]), L["w1"][:], hT[s][:], start=True, stop=True).then_inc(L["mm1"], 1)
                    if group := group_at(r, u, 2):
                        s = group[1] % 2
                        acc = by_j(banks[4 + group[1] % SLOTS])
                        pe.wait_ge(L["hid"], upto(*group))
                        if before := group_at(r, u, 2 + SLOTS):
                            pe.wait_ge(L["y"], upto(*before))
                        if L["norm"]:
                            te.matmul(acc, ones_bf[:], L["b2"], start=True, stop=False)
                        for j in range(J):
                            last = te.matmul(acc[:, j, :], hid[s][:, j, :], L["w2"][:], start=not L["norm"], stop=(not L["norm"] or j == J - 1))
                        last.then_inc(L["mm2"], 1)
                run(pe, step, 0, 2)

            def step_c(C, r, u):
                now, nxt, last = group_at(r, u, 0), group_at(r, u, -1), group_at(r, u, 1)
                if nxt and not C["any"]:
                    s = nxt[1] % SLOTS
                    pe.wait_ge(C["gathered"][s], slot_uses(*nxt) * (16 * 2 * K))
                    pe.wait_ge(C["att"][s], slot_uses(*nxt) * (16 * K))
                    for rows, b in ((xsrc, 0), (xdst, 1), (xatt, 2)):
                        for k in range(K):
                            ins = te.transpose(by_k(banks[b])[:, k, :], rows[s][:, k, :], ident)
                        ins.then_inc(C["edgeT"], 1)
                if now:
                    pe.wait_ge(C["in"][u], 16 * (now[0] + 1))
                    for j in range(J):
                        ins = te.transpose(by_j(banks[5])[:, j, :], xin[u][:, j, :], ident)
                    ins.then_inc(C["xT"], 1)
                if last:
                    acc = by_j(banks[7])
                    pe.wait_ge(C["hid"], upto(*last))
                    if before := group_at(r, u, 2):
                        pe.wait_ge(C["y"], upto(*before))
                    te.matmul(acc, ones_bf[:], brow_bf["b2"], start=True, stop=False)
                    for j in range(J):
                        ins = te.matmul(acc[:, j, :], hid[0][:, j, :], weights["W2"][:], start=False, stop=(j == J - 1))
                    ins.then_inc(C["w2"], 1)
                if now:
                    if C["any"]:
                        pe.wait_ge(C["res"][u], 16 * (now[0] + 1))
                        for j in range(J):
                            ins = te.transpose(by_j(banks[4])[:, j, :], xres[u][:, j, :], ident)
                        ins.then_inc(C["sumT"], 1)
                if nxt and not C["any"]:
                    pe.wait_ge(C["srcT"], upto(*nxt))
                    te.matmul(by_k(banks[0]), weights["Ws"][:], srcT[:], start=True, stop=False)
                    pe.wait_ge(C["dstT"], upto(*nxt))
                    te.matmul(by_k(banks[0]), weights["Wd"][:], dstT[:], start=False, stop=False)
                    pe.wait_ge(C["attT"], upto(*nxt))
                    te.matmul(by_k(banks[0]), weights["Wa"][:], attT[:], start=False, stop=True).then_inc(C["logits"], 1)
                    te.matmul(by_k(banks[1]), weights["Wm"][:], srcT[:], start=True, stop=True).then_inc(C["gatemm"], 1)
                if now:
                    pe.wait_ge(C["xTs"], upto(*now))
                    te.matmul(by_j(banks[6]), weights["W1x"][:], hT[0][:], start=True, stop=False)
                    if C["any"]:
                        pe.wait_ge(C["aggT"], upto(*now))
                        ins = te.matmul(by_j(banks[6]), weights["W1g"][:], aggT[:], start=False, stop=True)
                    else:
                        pe.wait_ge(C["msg"], upto(*now))
                        pe.wait_ge(C["built"], upto(*now))
                        for k, (p0, p1) in enumerate(SPANS):
                            ins = te.matmul(by_j(banks[6])[:, :, p0:p1], msg[:, k, :], sel[u % 2][:, :, p0:p1], start=False, stop=(k == K - 1))
                    ins.then_inc(C["w1"], 1)
                if nxt and not C["any"]:
                    pe.wait_ge(C["msgT"], upto(*nxt))
                    for k in range(K):
                        ins = te.matmul(by_k(banks[3])[:, k, :], msgT[:, k, :], weights["W1g"][:], start=True, stop=True)
                    ins.then_inc(C["msgmm"], 1)
            def layers(A, B, C):
                for L in (A, B):
                    if L["any"]:
                        edge_sums(L)
                    gin(L)
                    rows_stored(pe, L)
                if C["any"]:
                    edge_sums(C)
                run(pe, lambda r, u: step_c(C, r, u), 1, 1)

            run_layers(pe, layers)

        @block.scalar
        def _(act):
            a = nc.scalar
            def normed(group, n, L, value, final, done, scaled):
                if group is None:
                    return
                r, u = group
                ln = ln_of(u)
                if u % 2 == 0:
                    act.wait_ge(L["chain"], scaled * LINKS)
                if final:
                    buffer_free(group, L)
                for j in range(J):
                    into = outt[u % SLOTS][:, j, :] if final else norm1[:, u % SLOTS, j, :]
                    c = n * PAIR + (u % 2) * J + j
                    last = a.activation(into, value[:, j, :], ACT.Identity, bias=ln["off"][:, c:c + 1], scale=ln["rstd"][:, c:c + 1])
                last.then_inc(done, 1)

            def buffer_free(group, L):
                r, u = group
                if not isinstance(r, int) or number(r, u) >= SLOTS:
                    act.wait_ge(L["stored"][u % SLOTS], (slot_uses(r, u) - 1) * 16)

            def gin(L):
                def step(r, u):
                    if group := group_at(r, u, 1):
                        s = group[1] % 2
                        act.wait_ge(L["mm1"], upto(*group))
                        a.activation(hid[s][:], by_j(banks[2 + s]), ACT.Relu, bias=L["b1"][:, 0:1]).then_inc(L["hid"], 1)
                    if L["norm"]:
                        if now := group_at(r, u, 0):
                            act.wait_ge(L["agg"], upto(*now))
                            a.copy(hT[u % 2][:], by_j(banks[u % 2])).then_inc(L["hT"], 1)
                        if old := group_at(r, u, 7):
                            normed(old, 0, L, ysum[:, old[1]], True, L["out"], pairs_upto(old[0], old[1] + 1))
                    elif group := group_at(r, u, 4):
                        act.wait_ge(L["y"], upto(*group))
                        buffer_free(group, L)
                        a.activation(outt[group[1] % SLOTS][:], xres[group[1]][:], ACT.Relu).then_inc(L["out"], 1)
                run(act, step, 0, 7 if L["norm"] else 4)

            def edge_gates():
                with act.Fori(0, ROW) as t:
                    act.wait_ge(G["edgeT"], t + 1)
                    for into, b in ((srcT, 0), (dstT, 1), (attT, 2)):
                        ins = a.copy(into[:, 0, 0:ROWS], banks[b][:, 0:ROWS])
                    ins.then_inc(G["rowsT"], 1)
                    act.wait_ge(G["gatemm"], t + 1)
                    a.activation(gate[:, 0, 0:ROWS], banks[1][:, 0:ROWS], ACT.Sigmoid, bias=gate_bias[:, 0:1]).then_inc(G["gate"], 1)

            def step_c(C, r, u):
                now, nxt, last = group_at(r, u, 0), group_at(r, u, -1), group_at(r, u, 1)
                if last:
                    act.wait_ge(C["w1"], upto(*last))
                    a.activation(sig[:], by_j(banks[6]), ACT.Sigmoid, bias=bias["b1"][:, 0:1]).then_inc(C["sig"], 1)
                if now and not C["any"]:
                    act.wait_ge(C["msgmm"], upto(*now))
                    a.copy(msg[:], by_k(banks[3])).then_inc(C["msg"], 1)
                if nxt and not C["any"]:
                    act.wait_ge(C["edgeT"], upto(*nxt) * 3 - 2)
                    a.copy(srcT[:], by_k(banks[0])).then_inc(C["srcT"], 1)
                    act.wait_ge(C["edgeT"], upto(*nxt) * 3 - 1)
                    a.copy(dstT[:], by_k(banks[1])).then_inc(C["dstT"], 1)
                    act.wait_ge(C["edgeT"], upto(*nxt) * 3)
                    a.copy(attT[:], by_k(banks[2])).then_inc(C["attT"], 1)
                if now:
                    act.wait_ge(C["xT"], upto(*now))
                    a.copy(hT[0][:], by_j(banks[5])).then_inc(C["xTs"], 1)
                    if C["any"]:
                        act.wait_ge(C["sumT"], upto(*now))
                        a.copy(aggT[:], by_j(banks[4])).then_inc(C["aggT"], 1)
                chains = (r * BODY + u - 2) // 2 if isinstance(r, int) else r * (BODY // 2) + u // 2 - 1
                normed(group_at(r, u, 8), 1, C, y2[:, u % SLOTS], True, C["out"], chains)
                if nxt and not C["any"]:
                    act.wait_ge(C["logits"], upto(*nxt))
                    a.activation(gate[:], by_k(banks[0]), ACT.Sigmoid, bias=gate_bias[:, 0:1]).then_inc(C["gate"], 1)
                normed(group_at(r, u, 4), 0, C, y[:, u % SLOTS], False, C["norm"], chains)
            def layers(A, B, C):
                for L in (A, B):
                    if L["any"]:
                        act.wait_ge(G["turn"], turn(L, ROW))
                    gin(L)
                    rows_stored(act, L)
                if C["any"]:
                    edge_gates()
                    act.wait_ge(G["turn"], turn(C, ROW))
                run(act, lambda r, u: step_c(C, r, u), 1, 8)

            run_layers(act, layers)

        @block.gpsimd
        def _(pool):
            g = nc.gpsimd

            def by_index(dest, rows, index, done):
                g.indirect_dma_start(dest, None, rows, bass.IndirectOffsetOnAxis(ap=index, axis=0)).then_inc(done, 16)

            pool.wait_ge(v_setup, ready["row_i"])
            for half, c, edge_list in ((0, 0, dst), (1, 0, dst), (0, 1, src), (1, 1, src)):
                for b in range(BLOCKS):
                    at = half * BLOCKS + b
                    done = s_first if (half, c) == (0, 0) else s_rows[c]
                    by_index(lists_i[:, b, c, half * ROW:(half + 1) * ROW], edge_list.rearrange("(r c) -> r c", c=ROW), row_i[:, at:at + 1], done)

            count = [0]

            def step(ins):
                count[0] += 1
                ins.then_inc(pool_setup, 1)
                pool.wait_ge(pool_setup, count[0])

            pool.wait_ge(s_first, 16 * BLOCKS)
            for c in range(2):
                pool.wait_ge(s_rows[c], 16 * (c + 1) * BLOCKS)
            step(g.memset(ones_bf[:], 1.0))
            pool.wait_ge(s_wt, 16 * (len(weights) + len(cols) + 3 * len(rows3) + 3))
            step(g.tensor_tensor(gate_bias[:], bias["bs"][:], bias["bd"][:], ALU.add))
            step(g.tensor_tensor(gate_bias[:], gate_bias[:], bias["ba"][:], ALU.add))
            for part in range(3):
                rest = brow if part == 0 else brest
                step(g.tensor_copy(bpart[:], rest[:]))
                at = slice(32 * part, 32 * part + 1)
                step(g.tensor_copy(brow_all[at, :, :], bpart[at, :, :]))
                if part < 2:
                    step(g.tensor_tensor(brest[:], rest[:], bpart[:], ALU.subtract))
            assert count[0] == BIAS_STEPS

            def gather(group, L):
                if group is None:
                    return
                pool.wait_ge(L["index"], upto(*group))
                pool.sem_inc(pool_turn, 1)
                s = group[1] % SLOTS
                for rows, idx in ((xsrc, src_idx), (xdst, dst_idx))[:2 if L["no"] == 2 else 1]:
                    for k in range(K):
                        by_index(rows[s][:, k, :], L["x"], idx[s][:, k:k + 1], L["gathered"][s])

            def layer(L):
                for g in range(SLOTS):
                    gather((0, g), L)
                run(pool, lambda r, u: gather(group_at(r, u, -SLOTS), L), 0, 0, exact=True)

            def edge_sums(L):
                pool.wait_ge(G["filled"], 16 * (L["no"] + 1))
                pool.sem_inc(G["turn"], 1)
                with pool.Fori(0, ROW) as t:
                    n = tile_no(L, t)
                    pool.wait_ge(G["index"], n)
                    pool.sem_inc(pool_turn, 1)
                    by_index(xsrc[0][0:ROWS, 0, :], L["x"], src_idx[0][0:ROWS, 0:1], G["rows"])
                    if L["no"] == 2:
                        by_index(xdst[0][0:ROWS, 0, :], L["x"], dst_idx[0][0:ROWS, 0:1], G["rows"])
                    by_index(xres[0][0:ROWS, 0, :], sums[0:N, :], dst_idx[0][0:ROWS, 0:1], G["old"])
                    pool.wait_ge(G["keep"], n)
                    pool.wait_ge(G["new"], n)
                    pool.sem_inc(pool_turn, 1)
                    g.indirect_dma_start(sums, bass.IndirectOffsetOnAxis(ap=keep_i[:, 0:1], axis=0), y[0:ROWS, 0, 0, :], None).then_inc(G["scattered"], 16)
                    pool.wait_ge(G["scattered"], n * 16)
                    pool.sem_inc(G["turn"], 1)

            def layers(A, B, C):
                for L in (A, B, C):
                    if L["any"]:
                        edge_sums(L)
                    else:
                        layer(L)
                    if L is not C:
                        rows_stored(pool, L)

            run_layers(pool, layers)

        @block.sync
        def _(sp):
            by_row = dst.rearrange("(r c) -> r c", c=ROW)
            sp.dma_start(dst_rows[:], by_row).then_inc(s_dst, 16)
            sp.dma_start(consts[:], t["constants"]).then_inc(s_const, 16)
            sp.wait_ge(v_setup, ready["brow"])
            sp.dma_start(next_row[0:ROWS - 1, :], by_row[1:, 0:8]).then_inc(s_next, 16)
            for n in weights:
                sp.dma_start(weights[n][:], weight_src[n]).then_inc(s_wt, 16)
            for n in cols:
                sp.dma_start(bias[n][:], col_src[n].rearrange("(f o) -> f o", o=1)).then_inc(s_wt, 16)
            for k, n in enumerate(rows3):
                for p in range(0, PARTS, 32):
                    sp.dma_start(brow[p:p + 1, k, :], row_src[n].rearrange("(o f) -> o f", o=1)).then_inc(s_wt, 16)
            for tile, vec in ((gamma, t["L1_gnn_gamma"]), (beta, t["L1_gnn_beta"])):
                sp.dma_start(tile[:], vec.partition_broadcast(P).rearrange("p (o f) -> p o f", o=1).to_broadcast([P, J, D])).then_inc(s_wt, 16)
            sp.dma_start(b2a[:], t["L0_gnn_b2a"].partition_broadcast(P).rearrange("p (o f) -> p o f", o=1)).then_inc(s_wt, 16)

            def layer(L, load, ahead, target, lag):
                def step(r, u):
                    load(L, group_at(r, u, -ahead))
                    if group := group_at(r, u, lag):
                        if isinstance(r, int) and number(*group) == 1:
                            sp.wait_ge(L["stored"][0], 16)
                        sp.wait_ge(L["out"], upto(*group))
                        sp.dma_start(node_rows(target, *group), outt[group[1] % SLOTS][:]).then_inc(L["stored"][group[1] % SLOTS], 16)
                for g in range(ahead):
                    if g > 0 and not L["any"]:
                        sp.wait_ge(L["gathered"][(g - 1) % SLOTS], slot_uses(0, g - 1) * (16 * K * (2 if L["no"] == 2 else 1)))
                    load(L, (0, g))
                run(sp, step, 0, lag, exact=True, apart=2)
                rows_stored(sp, L)

            def load_a(A, group):
                if group is None:
                    return
                r, u = group
                if number(r, u) >= BODY if isinstance(r, int) else True:
                    sp.wait_ge(A["agg"], upto(r, u) - BODY)
                sp.dma_start(xin[u][:], node_rows(sums if A["any"] else x, r, u)).then_inc(A["in"][u], 16)

            def load_b(B, group):
                if group is None:
                    return
                r, u = group
                if number(r, u) >= BODY if isinstance(r, int) else True:
                    sp.wait_ge(B["y"], upto(r, u) - BODY)
                sp.dma_start(xin[u][:], node_rows(sums if B["any"] else h1, r, u)).then_inc(B["in"][u], 16)
                sp.dma_start(xres[u][:], node_rows(x, r, u)).then_inc(B["res"][u], 16)

            def load_c(C, group):
                if group is None:
                    return
                r, u = group
                if not C["any"] and (number(r, u) >= SLOTS if isinstance(r, int) else True):
                    sp.wait_ge(C["edgeT"], (upto(r, u) - SLOTS) * 3)
                for k in range(0 if C["any"] else K):
                    edge = sp.value_load(first_edge[0:1, bass.ds(number(r, u) * K + k, 1)], min_val=0, max_val=E - P)
                    sp.dma_start(xatt[u % SLOTS][:, k, :], attr[bass.ds(edge, P), :]).then_inc(C["att"][u % SLOTS], 16)
                if number(r, u) >= BODY if isinstance(r, int) else True:
                    sp.wait_ge(C["y2"], upto(r, u) - BODY)
                sp.dma_start(xin[u][:], node_rows(x1, r, u)).then_inc(C["in"][u], 16)
                if C["any"]:
                    sp.dma_start(xres[u][:], node_rows(sums, r, u)).then_inc(C["res"][u], 16)

            def edge_sums(L):
                if L["no"] == 2:
                    sp.wait_ge(G["zero"], 1)
                    zeros = norm1[0:ROWS, 0, 0:1, :].to_broadcast([ROWS, N // ROWS, D])
                    sp.dma_start(sums[0:N, :].rearrange("(p q) f -> p q f", p=ROWS), zeros).then_inc(G["filled"], 16)
                    with sp.Fori(0, ROW) as t:
                        sp.wait_ge(G["turn"], turn(L, t))
                        sp.dma_start(xatt[0][0:ROWS, 0:1, :], attr.rearrange("(p t) f -> p t f", t=ROW)[:, bass.ds(t, 1), :]).then_inc(G["att"], 16)
                else:
                    sp.dma_start(sums[0:N, :], L["x"]).then_inc(G["filled"], 16)
                sp.wait_ge(G["filled"], 16 * (L["no"] + 1))
                sp.wait_ge(G["turn"], turn(L, ROW))

            def layers(A, B, C):
                if A["any"]:
                    sp.dma_start(src_rows[:], src.rearrange("(r c) -> r c", c=ROW)).then_inc(s_any, 16)
                    sp.dma_start(pairs[:], t["pairs"]).then_inc(s_any, 16)
                for L, load, ahead, target, lag in ((A, load_a, 6, h1, 5), (B, load_b, 6, x1, 8), (C, load_c, SLOTS, out, 9)):
                    if L["any"]:
                        edge_sums(L)
                    layer(L, load, ahead, target, lag)

            run_layers(sp, layers)


_INS = ['x', 'src', 'dst', 'edge_attr_128',
        'L0_gnn_W1a', 'L0_gnn_b1a', 'L0_gnn_W2a', 'L0_gnn_b2a', 'L0_gnn_W1b', 'L0_gnn_b1b', 'L0_gnn_W2b', 'L0_gnn_b2b',
        'L1_gnn_Ws', 'L1_gnn_bs', 'L1_gnn_Wd', 'L1_gnn_bd', 'L1_gnn_Wa', 'L1_gnn_ba', 'L1_gnn_Wm', 'L1_gnn_bm',
        'L1_gnn_W1', 'L1_gnn_b1', 'L1_gnn_W2', 'L1_gnn_b2', 'L1_gnn_gamma', 'L1_gnn_beta']


def kernel(**inputs):
    import numpy as _np
    import concourse.bacc as _bacc
    from concourse import mybir as _mybir
    from concourse.bass_utils import run_bass_kernel_spmd as _run

    nc = _bacc.Bacc("TRN2", target_bir_lowering=False, num_devices=1)
    arrays, args = {}, {}
    given = {name: _np.ascontiguousarray(inputs[name]) for name in _INS}
    given["constants"] = constants()
    given["pairs"] = pair_constants()
    for name, a in given.items():
        arrays[f"in_{name}"] = a
        args[name] = nc.dram_tensor(f"in_{name}", a.shape, _mybir.dt.from_np(a.dtype), kind="ExternalInput").ap()
    out = nc.dram_tensor("out_0_dram", (N, D), F32, kind="ExternalOutput").ap()
    gnn_kernel(nc, args, out)
    r = _run(nc, [arrays], core_ids=[0])
    return r.results[0]["out_0_dram"]
```
